# Optimizing a Trainium2 kernel written in Bass

```python
import numpy as np
import jax
import jax.numpy as jnp

def _softmax(x, axis=-1):
    return jax.nn.softmax(x, axis=axis)

def _gelu(x):
    return jax.nn.gelu(x, approximate=True)

def _silu(x):
    return jax.nn.silu(x)

def _sigmoid(x):
    return jax.nn.sigmoid(x)

def _layernorm(x, axis=-1, eps=1e-05):
    m = jnp.mean(x, axis=axis, keepdims=True)
    v = jnp.var(x, axis=axis, keepdims=True)
    return (x - m) / jnp.sqrt(v + eps)

def _scatter_add(tgt, idx, src, axis=0):
    return tgt.at[idx].add(src)

def _segment_sum(src, seg, n):
    return jax.ops.segment_sum(src, seg, n)
kernel_name = 'mk_adj_resnorm_d2_adj_r2_e3c0b6'

def setup_inputs(seed: int=0):
    np.random.seed(seed)
    _w = jnp.asarray

    def _rec_inputs():
        import jax
        import jax.numpy as jnp
        _gk = jax.random.key(seed)
        x = -0.001003 + 1 * jax.random.normal(jax.random.fold_in(_gk, 1), (6144, 128), jnp.float32)
        _w = (1.0 + jnp.arange(6144, dtype=jnp.float32)) ** (-0.5)
        _w = _w / _w.mean()
        _pij = jnp.clip(0.000325521 * _w[:, None] * _w[None, :], 0.0, 1.0)
        _a = jax.random.uniform(jax.random.fold_in(_gk, 2), (6144, 6144)) < _pij
        adj = _a.astype(jnp.int32)
        return (x, adj)
    x, adj = _rec_inputs()

    def _L0_gnn_setup():
        import jax, jax.numpy as jnp
        import numpy as np
        M = 6144
        N = 6144
        D = 128
        TEMPERATURE = 0.07
        NEG_PAD = jnp.float32(-2 ** 32 + 1)
        key = jax.random.key(seed)
        k1, k2, k3, k4 = jax.random.split(key, 4)
        xx_anchor = jax.random.normal(k1, (M, D), dtype=jnp.float32)
        inp = jax.random.normal(k2, (N, D), dtype=jnp.float32)
        adj = (jax.random.uniform(k3, (M, N)) < 0.002).astype(jnp.int32)
        limit = jnp.sqrt(6.0 / (D + D)).astype(jnp.float32)
        weight = jax.random.uniform(k4, (D, D), minval=-limit, maxval=limit, dtype=jnp.float32)
        return {'xx_anchor': xx_anchor, 'input': inp, 'adj': adj, 'weight': weight}
    _L0_gnn_all = _L0_gnn_setup()
    _L0_gnn_in = {k: v for k, v in _L0_gnn_all.items() if k in ('input', 'weight')}
    del _L0_gnn_all

    def _L1_gnn_setup():
        import jax, jax.numpy as jnp
        import numpy as np
        ALPHA = 0.2
        NEG_BIG = -9000000000000000.0
        key = jax.random.key(seed)
        k1, k2, k3, k4 = jax.random.split(key, 4)
        N, F_IN, F_OUT = (4096, 128, 128)
        h = jax.random.normal(k1, (N, F_IN), dtype=jnp.float32)
        adj = jax.random.randint(k2, (N, N), 0, 2, dtype=jnp.int32)
        W = jax.random.normal(k3, (F_IN, F_OUT), dtype=jnp.float32) * (1.0 / np.sqrt(F_IN))
        a = jax.random.normal(k4, (2 * F_OUT, 1), dtype=jnp.float32) * (1.0 / np.sqrt(2 * F_OUT))
        return {'h': h, 'adj': adj, 'W': W, 'a': a}
    _L1_gnn_all = _L1_gnn_setup()
    _L1_gnn_in = {k: v for k, v in _L1_gnn_all.items() if k in ('W', 'a')}
    del _L1_gnn_all
    return {'x': x, 'adj': adj, 'L0_gnn_input': _L0_gnn_in['input'], 'L0_gnn_weight': _L0_gnn_in['weight'], 'L1_gnn_W': _L1_gnn_in['W'], 'L1_gnn_a': _L1_gnn_in['a']}

def reference(x, adj, L0_gnn_input, L0_gnn_weight, L1_gnn_W, L1_gnn_a):
    import jax
    import jax.numpy as jnp

    def _L0_gnn_ref(xx_anchor, input, adj, weight):
        import jax, jax.numpy as jnp
        import numpy as np
        M = 6144
        N = 6144
        D = 128
        TEMPERATURE = 0.07
        NEG_PAD = jnp.float32(-2 ** 32 + 1)
        anchor_adj = jnp.einsum('md,de,ne->mn', xx_anchor, weight, input)
        scores = jnp.where(adj > 0, anchor_adj, NEG_PAD)
        atten = jax.nn.softmax(scores / TEMPERATURE, axis=1)
        return atten @ input

    def _L1_gnn_ref(h, adj, W, a):
        import jax, jax.numpy as jnp
        import numpy as np
        ALPHA = 0.2
        NEG_BIG = -9000000000000000.0
        Wh = h @ W
        F_out = Wh.shape[1]
        a1 = a[:F_out, 0]
        a2 = a[F_out:, 0]
        e = (Wh @ a1)[:, None] + (Wh @ a2)[None, :]
        e = jnp.where(e >= 0, e, ALPHA * e)
        scores = jnp.where(adj > 0, e, NEG_BIG)
        attention = jax.nn.softmax(scores, axis=1)
        return attention @ Wh
    x = _layernorm(x + _L0_gnn_ref(x, L0_gnn_input, adj, L0_gnn_weight), axis=-1)
    x = _layernorm(x + _L1_gnn_ref(x, adj, L1_gnn_W, L1_gnn_a), axis=-1)
    return x

_drawn_inputs = setup_inputs


def setup_inputs(seed=0):
    import zlib

    import numpy as np

    out = dict(_drawn_inputs(seed))
    spreads = {}
    factors = {}
    for name, (base, spread) in spreads.items():
        noise = np.random.default_rng([zlib.crc32(name.encode()), seed]).standard_normal(out[name].shape)
        drawn = base * np.exp(spread * noise) if base else spread * noise
        out[name] = jnp.asarray(drawn.astype(out[name].dtype))
    for name, factor in factors.items():
        out[name] = (out[name] * factor).astype(out[name].dtype)
    return out
```

```python
from contextlib import ExitStack
from math import log

import concourse.bass as bass
from concourse import mybir

P = 128
W_SC = 1024
W_GR = 512
W_PC = 2048
SPLIT = 64.0
Q_SPLIT = 4.0
TEMPERATURE = 0.07
ALPHA = 0.2
EPS = 1e-5
P_SCALE = 4096.0
MASKED = -2.0 ** 100
QK_LEAD = 9
MASK_LEAD = 8
EXP_LEAD = 2
PV_LAG = 2

F32 = mybir.dt.float32
F16 = mybir.dt.float16
BF16 = mybir.dt.bfloat16
I32 = mybir.dt.int32
ALU = mybir.AluOpType
ACT = mybir.ActivationFunctionType
AX_X = mybir.AxisListType.X


def two_layer_graph_attention(nc, x, adj, inp, w0, w1, a, out):
    N, D = x.shape
    TILES = N // P
    CH = N // W_SC
    GR = N // W_GR
    PC = N // W_PC
    BLK = W_GR // P
    PAIRS = TILES // 2
    S_TOT = TILES * CH
    RING = 2 * CH
    CPP = W_PC // W_SC
    PIECES = TILES * PC
    CHAIN = 8
    assert D == P and TILES % 2 == 0

    with ExitStack() as ctx:
        def sb(name, shape, dt):
            return ctx.enter_context(nc.sbuf_tensor(name, shape, dt))

        def sem(name):
            return ctx.enter_context(nc.semaphore(name))

        adj_ring = sb("adj_ring", [P, PC, W_PC], I32)
        mask_ring = sb("mask_ring", [P, PC, W_PC], BF16)
        y = sb("y", [P, RING * W_SC], F32)
        keys = sb("keys", [P, N], F32)
        val = sb("val", [P, TILES, 2 * D], F16)
        qx = sb("qx", [P, TILES, D], F32)
        pt = sb("pt", [P, 4, 2, W_GR], F16)
        xres = sb("xres", [P, 2, D], F32)
        ident = sb("ident", [P, P], F32)
        w0_sb = sb("w0_sb", [P, D], F32)
        w1_sb = sb("w1_sb", [P, D + 1], F32)
        w1t = sb("w1t", [P, D], F32)
        a_sb = sb("a_sb", [P, 2], F32)
        wa2 = sb("wa2", [P, D], F32)
        ones = sb("ones", [P, D], F32)
        wa_sb = sb("wa_sb", [P, 2], F32)
        f1 = sb("f1", [P, TILES], F32)
        f1_now = sb("f1_now", [P, 2], F32)
        cmax = sb("cmax", [P, 2, CH], F32)
        rowmax = sb("rowmax", [P, 2], F32)
        f2_parts = sb("f2_parts", [96, N], BF16)
        part_sum = sb("part_sum", [96, P], BF16)
        ident16 = sb("ident16", [P, P], BF16)
        ebias = sb("ebias", [P, 2], F32)
        csum = sb("csum", [P, 2, CH], F32)
        rsum = sb("rsum", [P, 2, 4], F32)
        z = sb("z", [P, 2, D], F32)
        stats = sb("stats", [P, nc.vector.BN_STATS_DIM], F32)
        moments = sb("moments", [P, nc.vector.BN_AGGR_DIM], F32)
        row_var = sb("row_var", [P, TILES], F32)
        var = sb("var", [P, TILES], F32)
        std = sb("std", [P, TILES], F32)
        rstd = sb("rstd", [P, TILES], F32)

        ps_s = ctx.enter_context(nc.psum_tensor("ps_s", [P, 2, W_SC], F32))
        ps_t = ctx.enter_context(nc.psum_tensor("ps_t", [P, 2, W_GR], F32))
        ps_o = ctx.enter_context(nc.psum_tensor("ps_o", [P, 2, W_GR], F32))

        in_landed = [sem(f"inp_landed{i}") for i in range(4)]
        x_landed = [sem(f"x_landed{i}") for i in range(4)]
        w_landed = sem("weights_landed")
        ident_ready = sem("ident_ready")
        vhi_ready = sem("value_high_ready")
        vlo_ready = sem("value_low_ready")
        kt_t = sem("keys_transposed")
        kt_hi = sem("keys_high_ready")
        kt_lo = sem("keys_low_ready")
        xt_t = sem("x_transposed")
        xt_sb = sem("x_transposed_copied")
        q_mm = sem("query_product_ready")
        q_hi = sem("query_high_ready")
        q_lo = sem("query_low_ready")
        adj_landed = [sem(f"adj_landed{i}") for i in range(PC)]
        mask_ready = sem("mask_ready")
        pool_gate = sem("pool_gate")
        vec_gate = sem("vector_gate")
        scores_ready = sem("scores_ready")
        masked_ready = sem("masked_ready")
        rowmax_ready = sem("rowmax_ready")
        ebias_ready = sem("exp_bias_ready")
        relu_ready = sem("relu_ready")
        exp_ready = sem("exp_ready")
        transposed = sem("weights_transposed")
        hi_ready = sem("weight_high_ready")
        lo_ready = sem("weight_low_ready")
        pv_done = sem("value_product_done")
        out_taken = sem("output_taken")
        xres_landed = [sem(f"residual_landed{i}") for i in range(2)]
        chain = sem("row_chain")
        var_ready = sem("variance_ready")
        std_ready = sem("std_ready")
        rstd_ready = sem("rstd_ready")
        rows_ready = sem("rows_normalised")
        x1t_t = sem("rows_transposed")
        x1t_sb = sem("rows_transposed_copied")
        w_prep = sem("weight_prep_product")
        w_copy = sem("weight_prep_copied")
        f1_ready = sem("f1_ready")
        f1_picked = sem("f1_picked")
        wh_mm = sem("wh_product_ready")
        wh_hi = sem("wh_high_ready")
        wh_lo = sem("wh_low_ready")
        f2_mm = sem("f2_product_ready")
        f2_sb = sem("f2_copied")
        f2_split = sem("f2_split")
        stored = sem("stored")

        kt_hl = keys[:, :].bitcast(F16).rearrange("p (h n) -> p h n", h=2)
        q_hl = qx[:, :, :].bitcast(F16).rearrange("p t (h m) -> p t h m", h=2)
        in_nat = y[:, 0:N].rearrange("p (b d) -> p b d", d=D)
        x_nat = y[:, N:2 * N].rearrange("p (b d) -> p b d", d=D)
        x1t = y[:, 0:N]
        xt_tmp = [pt[:, i, :, :].rearrange("p h n -> p (h n)").bitcast(F32) for i in range(2)]
        x_dram = x.rearrange("(b p) d -> p b d", p=P)
        in_dram = inp.rearrange("(b p) d -> p b d", p=P)
        out_dram = out.rearrange("(b p) d -> p b d", p=P)
        adj_dram = adj.rearrange("(t p) (q n) -> t p q n", p=P, n=W_PC)
        QB = TILES // 4
        WHB = 3
        WHG = TILES // WHB

        def wait(eng, s, value):
            if not (isinstance(value, int) and value <= 0):
                eng.wait_ge(s, value)

        def y_chunk(c):
            return y[:, (c % RING) * W_SC:(c % RING + 1) * W_SC]

        block = ctx.enter_context(nc.Block())

        @block.sync
        def _(sp):
            sp.dma_start(w0_sb[:, :], w0).then_inc(w_landed, 16)
            for i in range(4):
                r = slice(i * QB, (i + 1) * QB)
                sp.dma_start(in_nat[:, r, :], in_dram[:, r, :]).then_inc(in_landed[i], 16)
                sp.dma_start(x_nat[:, r, :], x_dram[:, r, :]).then_inc(x_landed[i], 16)
            sp.dma_start(w1_sb[:, 0:D], w1).then_inc(w_landed, 16)
            for h in range(2):
                sp.dma_start(a_sb[:, h:h + 1], a[h * D:(h + 1) * D, :]).then_inc(w_landed, 16)

            def adjacency(layer, u):
                for j in range(2 * PC):
                    q = layer * PIECES + 2 * PC * u + j
                    wait(sp, mask_ready, q - PC + 1)
                    sp.dma_start(adj_ring[:, j % PC, :], adj_dram[2 * u + j // PC, :, j % PC, :]
                                 ).then_inc(adj_landed[j % PC], 16)

            adjacency(0, 0)
            with sp.Fori(1, PAIRS) as u:
                adjacency(0, u)
            with sp.Fori(0, PAIRS) as u:
                adjacency(1, u)
            for i in range(4):
                r = slice(i * QB, (i + 1) * QB)
                sp.wait_ge(rows_ready, 4 + i + 1)
                sp.dma_start(out_dram[:, r, :], qx[:, r, :]).then_inc(stored, 16)
            sp.wait_ge(stored, 64)

        @block.gpsimd
        def _(pool):
            nc.gpsimd.memset(ident[:, :], 0.0).then_inc(ident_ready, 1)
            nc.gpsimd.memset(ones[:, :], 1.0).then_inc(ident_ready, 1)
            pool.wait_ge(ident_ready, 2)
            nc.gpsimd.affine_select(out=ident[:, :], in_=ident[:, :], compare_op=ALU.not_equal, fill=1.0, base=0,
                                    pattern=[[-1, P]], channel_multiplier=1).then_inc(ident_ready, 1)
            pool.wait_ge(ident_ready, 3)
            nc.gpsimd.tensor_copy(ident16[:, :], ident[:, :]).then_inc(ident_ready, 1)
            nc.gpsimd.memset(part_sum[:, :], 0.0).then_inc(ident_ready, 1)
            pool.wait_ge(ident_ready, 5)
            for part in range(3):
                nc.gpsimd.memset(part_sum[32 * part:32 * part + 1, :], 1.0).then_inc(ident_ready, 1)
                pool.wait_ge(ident_ready, 6 + part)
            for i in range(4):
                r = slice(i * QB, (i + 1) * QB)
                pool.wait_ge(in_landed[i], 16)
                nc.gpsimd.tensor_scalar(val[:, r, 0:D], in_nat[:, r, :], SPLIT, None, ALU.mult).then_inc(vhi_ready, 1)

            def mask_piece(layer, u, j):
                q = layer * PIECES + 2 * PC * u + j
                pool.wait_ge(adj_landed[j % PC], 16 * (layer * TILES + 2 * u + j // PC + 1))
                if layer == 0 or (isinstance(u, int) and j < PC):
                    wait(pool, masked_ready, CPP * (q - PC + 1))
                else:
                    pool.wait_ge(scores_ready, CPP * (q - PC + 1))
                pool.sem_inc(pool_gate, 1)
                nc.gpsimd.tensor_scalar(mask_ring[:, j % PC, :], adj_ring[:, j % PC, :], 0.0, MASKED,
                                        ALU.is_le, ALU.mult).then_inc(mask_ready, 1)

            def relu_piece(u, j):
                t = 2 * u + j // PC
                for c in range(CPP):
                    i = CPP * j + c
                    pool.wait_ge(transposed, 2 * (S_TOT + RING * u + i - RING + 1))
                    cols = slice((i % CH) * W_SC, (i % CH + 1) * W_SC)
                    pool.sem_inc(pool_gate, 1)
                    nc.gpsimd.tensor_scalar(y_chunk(i), keys[:, cols], f1_now[:, j // PC:j // PC + 1], 0.0,
                                            ALU.add, ALU.max).then_inc(relu_ready, 1)

            def relus(u):
                for j in range(2 * PC):
                    mask_piece(1, u, j)
                    if j % PC == 0:
                        pool.wait_ge(f1_ready, WHG)
                        wait(pool, relu_ready, CH * (2 * u + j // PC - 1))
                        nc.gpsimd.tensor_copy(f1_now[:, j // PC:j // PC + 1], f1[:, bass.ds(2 * u + j // PC, 1)]
                                              ).then_inc(f1_picked, 1)
                        pool.wait_ge(f1_picked, 2 * u + j // PC + 1)
                        if isinstance(u, int):
                            pool.wait_ge(f2_split, 4)
                    relu_piece(u, j)

            for j in range(2 * PC):
                mask_piece(0, 0, j)
            with pool.Fori(1, PAIRS) as u:
                for j in range(2 * PC):
                    mask_piece(0, u, j)
            relus(0)
            with pool.Fori(1, PAIRS) as u:
                relus(u)

        @block.tensor
        def _(pe):
            def four_transposes(dst, src, g):
                for b in range(BLK):
                    last = nc.tensor.transpose(dst[:, b * P:(b + 1) * P], src[:, g * W_GR + b * P:g * W_GR + (b + 1) * P],
                                               ident[:, :])
                return last

            pe.wait_ge(ident_ready, 8)
            pe.wait_ge(w_landed, 64)
            for g in range(GR + 1):
                if g < GR:
                    pe.wait_ge(in_landed[g * BLK // QB], 16)
                    if g >= 2:
                        pe.wait_ge(kt_lo, g - 1)
                    four_transposes(ps_t[:, g % 2, :], y[:, 0:N], g).then_inc(kt_t, 1)
                    pe.wait_ge(x_landed[g * BLK // QB], 16)
                    if g >= 2:
                        pe.wait_ge(xt_sb, g - 1)
                    four_transposes(ps_s[:, 0, (g % 2) * W_GR:(g % 2 + 1) * W_GR], y[:, N:2 * N], g).then_inc(xt_t, 1)
                if g >= 1:
                    h = g - 1
                    pe.wait_ge(xt_sb, h + 1)
                    if h >= 2:
                        pe.wait_ge(q_lo, h - 1)
                    nc.tensor.matmul(ps_s[:, 1, (h % 2) * W_GR:(h % 2 + 1) * W_GR], w0_sb[:, :], xt_tmp[h % 2],
                                     start=True, stop=True).then_inc(q_mm, 1)
            pe.wait_ge(kt_lo, GR)
            nc.tensor.transpose(ps_t[:, 0, 0:P], w1_sb[:, 0:D], ident[:, :]).then_inc(w_prep, 1)
            pe.wait_ge(w_copy, 1)
            nc.tensor.matmul(ps_t[:, 1, 0:2], w1t[:, :], a_sb[:, :], start=True, stop=True).then_inc(w_prep, 1)
            pe.wait_ge(w_copy, 2)
            pe.wait_ge(q_lo, GR)

            def qk_half(n, i, h, tile):
                bank = ps_s[:, i % 2, h * W_GR:(h + 1) * W_GR]
                cols = slice((i % CH) * W_SC + h * W_GR, (i % CH) * W_SC + (h + 1) * W_GR)
                if h == 0:
                    wait(pe, masked_ready, n - 1)
                qh = q_hl[:, bass.ds(tile, 1), 0, :].rearrange("p o m -> p (o m)")
                ql = q_hl[:, bass.ds(tile, 1), 1, :].rearrange("p o m -> p (o m)")
                nc.tensor.matmul(bank, qh, kt_hl[:, 0, cols], start=True, stop=False)
                nc.tensor.matmul(bank, qh, kt_hl[:, 1, cols], start=False, stop=False)
                last = nc.tensor.matmul(bank, ql, kt_hl[:, 0, cols], start=False, stop=True)
                if h == 1:
                    last.then_inc(scores_ready, 1)

            def logit_half(n, i, h, tile):
                bank = ps_s[:, i % 2, h * W_GR:(h + 1) * W_GR]
                c = i % CH
                cols = slice(c * W_SC + h * W_GR, c * W_SC + (h + 1) * W_GR)
                piece, at = c // CPP, (c % CPP) * W_SC + h * W_GR
                if h == 0:
                    pe.wait_ge(masked_ready, n - 1)
                    pe.wait_ge(mask_ready, tile * PC + piece + 1)
                nc.tensor.matmul(bank, ident16[:, :], mask_ring[:, piece, at:at + W_GR], start=True, stop=False)
                last = nc.tensor.matmul(bank, part_sum[:, :], f2_parts[:, cols], start=False, stop=True)
                if h == 1:
                    last.then_inc(scores_ready, 1)

            def value_product(k, i):
                pe.wait_ge(lo_ready, k + 1)
                first, fin = i % GR == 0, i % GR == GR - 1
                o = ps_o[:, (i // GR) % 2, 0:2 * D]
                for b in range(BLK):
                    v = val[:, (i % GR) * BLK + b, :]
                    nc.tensor.matmul(o, pt[:, i % 4, 0, b * P:(b + 1) * P], v, start=first and b == 0, stop=False)
                    last = nc.tensor.matmul(o[:, 0:D], pt[:, i % 4, 1, b * P:(b + 1) * P], v[:, 0:D], start=False,
                                            stop=fin and b == BLK - 1)
                last.then_inc(pv_done, 1)

            def body(layer, u, first, last):
                s0, k0 = layer * S_TOT + RING * u, 2 * (layer * S_TOT + RING * u)
                for i in range(RING):
                    for h in range(2):
                        if not (last and i + QK_LEAD >= RING):
                            ahead = qk_half if layer == 0 else logit_half
                            ahead(s0 + i + QK_LEAD, i + QK_LEAD, h, layer * TILES + 2 * u + (i + QK_LEAD) // CH)
                        g = 2 * i + h
                        pe.wait_ge(exp_ready, s0 + i + 1)
                        wait(pe, lo_ready, k0 + g - 1)
                        four_transposes(ps_t[:, g % 2, :], y[:, :], g).then_inc(transposed, 1)
                        if not (first and g < PV_LAG):
                            j = (g - PV_LAG) % (2 * GR)
                            if j % GR == 0:
                                wait(pe, out_taken, layer * TILES + 2 * u + (g - PV_LAG) // GR - 1)
                            value_product(k0 + g - PV_LAG, j)

            for n in range(QK_LEAD):
                for h in range(2):
                    qk_half(n, n, h, n // CH)
            body(0, 0, True, False)
            with pe.Fori(1, PAIRS - 1) as u:
                body(0, u, False, False)
            body(0, PAIRS - 1, False, True)
            for j in range(2 * GR - PV_LAG, 2 * GR):
                value_product(2 * S_TOT - 2 * GR + j, j)

            for g in range(GR):
                pe.wait_ge(rows_ready, g * BLK // QB + 1)
                if g >= 2:
                    pe.wait_ge(x1t_sb, g - 1)
                four_transposes(ps_t[:, g % 2, :], qx[:, :, :].rearrange("p t d -> p (t d)"), g).then_inc(x1t_t, 1)
            for g in range(GR):
                pe.wait_ge(x1t_sb, g + 1)
                if g >= 2:
                    pe.wait_ge(f2_sb, g - 1)
                nc.tensor.matmul(ps_s[:, 0, (g % 2) * W_GR:(g % 2 + 1) * W_GR], wa2[:, :], x1t[:, g * W_GR:(g + 1) * W_GR],
                                 start=True, stop=True).then_inc(f2_mm, 1)
            for g in range(WHG):
                if g >= 2:
                    pe.wait_ge(wh_lo, g - 1)
                for b in range(WHB):
                    t = g * WHB + b
                    last = nc.tensor.matmul(ps_s[:, 1, (g % 2) * W_GR + b * (D + 1):(g % 2) * W_GR + (b + 1) * (D + 1)],
                                            x1t[:, t * P:(t + 1) * P], w1_sb[:, :], start=b == 0, stop=b == WHB - 1)
                last.then_inc(wh_mm, 1)
            pe.wait_ge(f2_split, 4)
            pe.wait_ge(wh_lo, WHG)
            for n in range(QK_LEAD):
                for h in range(2):
                    logit_half(S_TOT + n, n, h, TILES + n // CH)
            body(1, 0, True, False)
            with pe.Fori(1, PAIRS - 1) as u:
                body(1, u, False, False)
            body(1, PAIRS - 1, False, True)
            for j in range(2 * GR - PV_LAG, 2 * GR):
                value_product(4 * S_TOT - 2 * GR + j, j)

        @block.scalar
        def _(act):
            for g in range(GR):
                act.wait_ge(kt_t, g + 1)
                nc.scalar.activation(kt_hl[:, 0, g * W_GR:(g + 1) * W_GR], ps_t[:, g % 2, :], ACT.Copy, scale=SPLIT
                                     ).then_inc(kt_hi, 1)
                act.wait_ge(xt_t, g + 1)
                if g >= 2:
                    act.wait_ge(q_mm, g - 1)
                nc.scalar.activation(xt_tmp[g % 2], ps_s[:, 0, (g % 2) * W_GR:(g % 2 + 1) * W_GR], ACT.Copy
                                     ).then_inc(xt_sb, 1)
                act.wait_ge(q_mm, g + 1)
                nc.scalar.activation(q_hl[:, g * BLK:(g + 1) * BLK, 0, :],
                                     ps_s[:, 1, (g % 2) * W_GR:(g % 2 + 1) * W_GR].rearrange("p (t m) -> p t m", m=P),
                                     ACT.Copy, scale=Q_SPLIT / TEMPERATURE).then_inc(q_hi, 1)
            act.wait_ge(w_prep, 1)
            nc.scalar.activation(w1t[:, :], ps_t[:, 0, 0:P], ACT.Copy).then_inc(w_copy, 1)

            def high(k, i):
                act.wait_ge(transposed, k + 1)
                wait(act, pv_done, k - 3)
                nc.scalar.activation(pt[:, i % 4, 0, :], ps_t[:, i % 2, :], ACT.Copy).then_inc(hi_ready, 1)

            def exponential(layer, n, i, tile):
                slot = (i // CH) % 2
                if i % CH == 0:
                    act.wait_ge(rowmax_ready, tile + 1)
                    nc.scalar.activation(ebias[:, slot:slot + 1], rowmax[:, slot:slot + 1], ACT.Copy, bias=log(P_SCALE),
                                         scale=-1.0 / (SPLIT * Q_SPLIT) if layer == 0 else -1.0).then_inc(ebias_ready, 1)
                    act.wait_ge(ebias_ready, tile + 1)
                nc.scalar.activation(y_chunk(i), y_chunk(i), ACT.Exp, bias=ebias[:, slot:slot + 1],
                                     scale=1.0 / (SPLIT * Q_SPLIT) if layer == 0 else 1.0,
                                     accum_out=csum[:, slot, i % CH:i % CH + 1]).then_inc(exp_ready, 1)

            def residual(tile, slot):
                wait(act, out_taken, tile - 1)
                act.dma_start(xres[:, slot, :], x_dram[:, bass.ds(tile, 1), :].rearrange("p o d -> p (o d)")
                              ).then_inc(xres_landed[slot], 16)

            def body(layer, u, last):
                s0 = layer * S_TOT + RING * u
                for i in range(RING):
                    high(2 * (s0 + i), 2 * i)
                    if layer == 0 and i % CH == 3:
                        residual(2 * u + i // CH, i // CH)
                    if not (last and i + EXP_LEAD >= RING):
                        exponential(layer, s0 + i + EXP_LEAD, i + EXP_LEAD, layer * TILES + 2 * u + (i + EXP_LEAD) // CH)
                    high(2 * (s0 + i) + 1, 2 * i + 1)

            for n in range(EXP_LEAD):
                exponential(0, n, n, 0)
            body(0, 0, False)
            with act.Fori(1, PAIRS - 1) as u:
                body(0, u, False)
            body(0, PAIRS - 1, True)

            def deviation(layer):
                act.wait_ge(var_ready, layer + 1)
                nc.scalar.activation(std[:, :], var[:, :], ACT.Sqrt).then_inc(std_ready, 1)

            deviation(0)
            for g in range(GR):
                act.wait_ge(x1t_t, g + 1)
                nc.scalar.activation(x1t[:, g * W_GR:(g + 1) * W_GR], ps_t[:, g % 2, :], ACT.Copy).then_inc(x1t_sb, 1)
            for g in range(GR):
                act.wait_ge(f2_mm, g + 1)
                nc.scalar.activation(keys[:, g * W_GR:(g + 1) * W_GR], ps_s[:, 0, (g % 2) * W_GR:(g % 2 + 1) * W_GR],
                                     ACT.Copy, scale=1.0 - ALPHA).then_inc(f2_sb, 1)
            act.wait_ge(f2_sb, GR)
            nc.scalar.activation(f2_parts[:, :], keys[0:96, :], ACT.Copy, scale=ALPHA / (1.0 - ALPHA)).then_inc(f2_split, 1)
            for g in range(WHG):
                act.wait_ge(wh_mm, g + 1)
                wh = ps_s[:, 1, (g % 2) * W_GR:(g % 2) * W_GR + WHB * (D + 1)].rearrange("p (b d) -> p b d", b=WHB)
                nc.scalar.activation(f1[:, g * WHB:(g + 1) * WHB], wh[:, :, D], ACT.Copy, scale=1.0 - ALPHA).then_inc(f1_ready, 1)
                nc.scalar.activation(val[:, g * WHB:(g + 1) * WHB, 0:D], wh[:, :, 0:D], ACT.Copy, scale=SPLIT
                                     ).then_inc(wh_hi, 1)
            for n in range(EXP_LEAD):
                exponential(1, S_TOT + n, n, TILES)
            body(1, 0, False)
            with act.Fori(1, PAIRS - 1) as u:
                body(1, u, False)
            body(1, PAIRS - 1, True)
            deviation(1)

        @block.vector
        def _(dve):
            for g in range(GR):
                dve.wait_ge(kt_hi, g + 1)
                nc.vector.scalar_tensor_tensor(out=kt_hl[:, 1, g * W_GR:(g + 1) * W_GR], in0=ps_t[:, g % 2, :], scalar=SPLIT,
                                               in1=kt_hl[:, 0, g * W_GR:(g + 1) * W_GR], op0=ALU.mult,
                                               op1=ALU.subtract).then_inc(kt_lo, 1)
                dve.wait_ge(q_hi, g + 1)
                nc.vector.scalar_tensor_tensor(
                    out=q_hl[:, g * BLK:(g + 1) * BLK, 1, :],
                    in0=ps_s[:, 1, (g % 2) * W_GR:(g % 2 + 1) * W_GR].rearrange("p (t m) -> p t m", m=P),
                    scalar=Q_SPLIT / TEMPERATURE, in1=q_hl[:, g * BLK:(g + 1) * BLK, 0, :], op0=ALU.mult,
                    op1=ALU.subtract).then_inc(q_lo, 1)
            for i in range(4):
                r = slice(i * QB, (i + 1) * QB)
                dve.wait_ge(vhi_ready, i + 1)
                nc.vector.scalar_tensor_tensor(out=val[:, r, D:2 * D], in0=in_nat[:, r, :], scalar=SPLIT,
                                               in1=val[:, r, 0:D], op0=ALU.mult, op1=ALU.subtract
                                               ).then_inc(vlo_ready, 1)
            dve.wait_ge(vlo_ready, 4)
            dve.wait_ge(w_prep, 2)
            nc.vector.tensor_copy(w1_sb[:, D:D + 1], ps_t[:, 1, 0:1])
            nc.vector.tensor_copy(wa_sb[:, :], ps_t[:, 1, 0:2]).then_inc(w_copy, 1)
            dve.wait_ge(w_copy, 2)
            nc.vector.tensor_scalar(wa2[:, :], ones[:, :], wa_sb[:, 1:2], None, ALU.mult).then_inc(w_copy, 1)

            def mask_chunk(layer, n, i, tile):
                c, slot, piece = i % CH, (i // CH) % 2, (i % CH) // CPP
                m = mask_ring[:, piece, (c % CPP) * W_SC:(c % CPP + 1) * W_SC]
                dve.wait_ge(scores_ready, n + 1)
                if layer == 0:
                    if c % CPP == 0:
                        dve.wait_ge(mask_ready, tile * PC + piece + 1)
                    wait(dve, transposed, 2 * (n - RING + 1))
                    add = m
                else:
                    dve.wait_ge(relu_ready, n - S_TOT + 1)
                    add = y_chunk(i)
                dve.sem_inc(vec_gate, 1)
                nc.vector.tensor_tensor_reduce(out=y_chunk(i), in0=ps_s[:, i % 2, :], in1=add, scale=1.0, scalar=-3.0e38,
                                               op0=ALU.add, op1=ALU.max, accum_out=cmax[:, slot, c:c + 1]
                                               ).then_inc(masked_ready, 1)
                if c == CH - 1:
                    dve.wait_ge(masked_ready, n + 1)
                    nc.vector.reduce_max(rowmax[:, slot:slot + 1], cmax[:, slot, :], AX_X).then_inc(rowmax_ready, 1)

            def low(k, i):
                dve.wait_ge(hi_ready, k + 1)
                nc.vector.tensor_tensor(pt[:, i % 4, 1, :], ps_t[:, i % 2, :], pt[:, i % 4, 0, :], ALU.subtract
                                        ).then_inc(lo_ready, 1)

            def rows(layer, t, slot):
                at = layer * TILES + t
                done = CHAIN * at
                dve.wait_ge(exp_ready, CH * (at + 1))
                nc.vector.reduce_sum(rsum[:, slot, 0:1], csum[:, slot, :], AX_X).then_inc(chain, 1)
                dve.wait_ge(chain, done + 1)
                nc.vector.tensor_scalar(rsum[:, slot, 1:2], rsum[:, slot, 0:1], SPLIT, None, ALU.mult).then_inc(chain, 1)
                dve.wait_ge(chain, done + 2)
                nc.vector.reciprocal(rsum[:, slot, 2:3], rsum[:, slot, 1:2]).then_inc(chain, 1)
                dve.wait_ge(chain, done + 3)
                dve.wait_ge(pv_done, GR * (at + 1))
                row = qx[:, bass.ds(t, 1), :].rearrange("p o d -> p (o d)")
                if layer == 0:
                    dve.wait_ge(xres_landed[slot], (t - slot) * 8 + 16)
                res = xres[:, slot, :] if layer == 0 else row
                nc.vector.scalar_tensor_tensor(out=z[:, 0, :], in0=ps_o[:, slot, 0:D], scalar=rsum[:, slot, 2:3], in1=res,
                                               op0=ALU.mult, op1=ALU.add).then_inc(chain, 1)
                dve.wait_ge(chain, done + 4)
                nc.vector.scalar_tensor_tensor(out=z[:, 1, :], in0=ps_o[:, slot, D:2 * D], scalar=rsum[:, slot, 2:3],
                                               in1=z[:, 0, :], op0=ALU.mult, op1=ALU.add).then_inc(out_taken, 1)
                dve.wait_ge(out_taken, at + 1)
                nc.vector.bn_stats(stats[:, :], z[:, 1, :]).then_inc(chain, 1)
                dve.wait_ge(chain, done + 5)
                dve.sem_inc(vec_gate, 1)
                nc.vector.bn_aggr(moments[:, :], stats[:, :]).then_inc(chain, 1)
                dve.wait_ge(chain, done + 6)
                nc.vector.tensor_scalar(row, z[:, 1, :], moments[:, 0:1], None, ALU.subtract).then_inc(chain, 1)
                nc.vector.tensor_copy(row_var[:, bass.ds(t, 1)], moments[:, 1:2]).then_inc(chain, 1)

            def body(layer, u, first, last):
                s0, t0 = layer * S_TOT + RING * u, layer * TILES + 2 * u
                for i in range(RING):
                    low(2 * (s0 + i), 2 * i)
                    if not (last and i + MASK_LEAD >= RING):
                        mask_chunk(layer, s0 + i + MASK_LEAD, i + MASK_LEAD, t0 + (i + MASK_LEAD) // CH)
                    low(2 * (s0 + i) + 1, 2 * i + 1)
                    if i % CH == 1 and not (first and i == 1):
                        rows(layer, 2 * u + i // CH - 1, (i // CH + 1) % 2)

            def normalise(layer):
                dve.wait_ge(chain, CHAIN * TILES * (layer + 1))
                nc.vector.tensor_scalar(var[:, :], row_var[:, :], EPS, None, ALU.add).then_inc(var_ready, 1)
                dve.wait_ge(std_ready, layer + 1)
                nc.vector.reciprocal(rstd[:, :], std[:, :]).then_inc(rstd_ready, 1)
                dve.wait_ge(rstd_ready, layer + 1)
                for i in range(4):
                    r = slice(i * QB, (i + 1) * QB)
                    nc.vector.tensor_tensor(qx[:, r, :], qx[:, r, :], rstd[:, r].unsqueeze(2).to_broadcast([P, QB, D]),
                                            ALU.mult).then_inc(rows_ready, 1)

            for n in range(MASK_LEAD):
                mask_chunk(0, n, n, n // CH)
            body(0, 0, True, False)
            with dve.Fori(1, PAIRS - 1) as u:
                body(0, u, False, False)
            body(0, PAIRS - 1, False, True)
            rows(0, TILES - 1, 1)
            normalise(0)
            for g in range(WHG):
                dve.wait_ge(wh_hi, g + 1)
                wh = ps_s[:, 1, (g % 2) * W_GR:(g % 2) * W_GR + WHB * (D + 1)].rearrange("p (b d) -> p b d", b=WHB)
                nc.vector.scalar_tensor_tensor(out=val[:, g * WHB:(g + 1) * WHB, D:2 * D], in0=wh[:, :, 0:D], scalar=SPLIT,
                                               in1=val[:, g * WHB:(g + 1) * WHB, 0:D], op0=ALU.mult,
                                               op1=ALU.subtract).then_inc(wh_lo, 1)
            dve.wait_ge(f2_split, 1)
            nc.vector.scalar_tensor_tensor(out=y[0:96, N:2 * N], in0=keys[0:96, :], scalar=ALPHA / (1.0 - ALPHA),
                                           in1=f2_parts[:, :], op0=ALU.mult, op1=ALU.subtract).then_inc(f2_split, 1)
            dve.wait_ge(f2_split, 2)
            for part in (1, 2):
                r = slice(32 * part, 32 * part + 32)
                last = nc.vector.tensor_copy(f2_parts[r, :], y[r, N:2 * N])
            last.then_inc(f2_split, 1)
            dve.wait_ge(f2_split, 3)
            nc.vector.tensor_tensor(f2_parts[64:96, :], y[64:96, N:2 * N], f2_parts[64:96, :], ALU.subtract
                                    ).then_inc(f2_split, 1)
            for n in range(MASK_LEAD):
                mask_chunk(1, S_TOT + n, n, TILES + n // CH)
            body(1, 0, True, False)
            with dve.Fori(1, PAIRS - 1) as u:
                body(1, u, False, False)
            body(1, PAIRS - 1, False, True)
            rows(1, TILES - 1, 1)
            normalise(1)


_INS = ['x', 'adj', 'L0_gnn_input', 'L0_gnn_weight', 'L1_gnn_W', 'L1_gnn_a']


def kernel(**inputs):
    import numpy as _np
    import concourse.bacc as _bacc
    from concourse import mybir as _mybir
    from concourse.bass_utils import run_bass_kernel_spmd as _run

    nc = _bacc.Bacc("TRN2", target_bir_lowering=False, num_devices=1)
    arrays, args = {}, []
    for name in _INS:
        arr = _np.ascontiguousarray(inputs[name])
        arrays[f"in_{name}_dram"] = arr
        args.append(nc.dram_tensor(f"in_{name}_dram", arr.shape, _mybir.dt.from_np(arr.dtype), kind="ExternalInput").ap())
    shape = inputs['x'].shape
    out = nc.dram_tensor("out_0_dram", shape, _mybir.dt.from_np(_np.dtype('float32')), kind="ExternalOutput").ap()
    two_layer_graph_attention(nc, *args, out)
    r = _run(nc, [arrays], core_ids=[0])
    return r.results[0]["out_0_dram"]
```

```python
from contextlib import ExitStack
from math import log

import concourse.bass as bass
from concourse import mybir

P = 128
W_SC = 1024
W_GR = 512
W_PC = 2048
SPLIT = 64.0
Q_SPLIT = 4.0
TEMPERATURE = 0.07
ALPHA = 0.2
EPS = 1e-5
P_SCALE = 4096.0
MASKED = -2.0 ** 100
QK_LEAD = 9
MASK_LEAD = 8
EXP_LEAD = 2
RELU_LEAD = (9, 10)
PV_LAG = 2

F32 = mybir.dt.float32
F16 = mybir.dt.float16
BF16 = mybir.dt.bfloat16
I32 = mybir.dt.int32
ALU = mybir.AluOpType
ACT = mybir.ActivationFunctionType
AX_X = mybir.AxisListType.X


def two_layer_graph_attention(nc, x, adj, inp, w0, w1, a, out):
    N, D = x.shape
    TILES = N // P
    CH = N // W_SC
    GR = N // W_GR
    PC = N // W_PC
    BLK = W_GR // P
    PAIRS = TILES // 2
    S_TOT = TILES * CH
    RING = 2 * CH
    CPP = W_PC // W_SC
    VEC_PIECE = PC - 1
    POOL_L0 = TILES * (PC - 1)
    CHAIN = 9
    OUT_TAKEN = 5
    assert D == P and TILES % 2 == 0

    with ExitStack() as ctx:
        def sb(name, shape, dt):
            return ctx.enter_context(nc.sbuf_tensor(name, shape, dt))

        def sem(name):
            return ctx.enter_context(nc.semaphore(name))

        adj_ring = sb("adj_ring", [P, PC, W_PC], I32)
        mask_ring = sb("mask_ring", [P, PC, W_PC], BF16)
        y = sb("y", [P, RING * W_SC], F32)
        keys = sb("keys", [P, N], F32)
        val = sb("val", [P, TILES, 2 * D], F16)
        qx = sb("qx", [P, TILES, D], F32)
        pt = sb("pt", [P, 4, 2, W_GR], F16)
        xres = sb("xres", [P, 2, D], F32)
        ident = sb("ident", [P, P], F32)
        w0_sb = sb("w0_sb", [P, D], F32)
        w1_sb = sb("w1_sb", [P, D + 1], F32)
        w1t = sb("w1t", [P, D], F32)
        a_sb = sb("a_sb", [P, 2], F32)
        wa2 = sb("wa2", [P, D], F32)
        ones = sb("ones", [P, D], F32)
        wa_sb = sb("wa_sb", [P, 2], F32)
        f1 = sb("f1", [P, TILES], F32)
        cmax = sb("cmax", [P, 2, CH], F32)
        rowmax = sb("rowmax", [P, 2], F32)
        f2_parts = sb("f2_parts", [96, N], BF16)
        part_sum = sb("part_sum", [96, P], BF16)
        ident_masked = sb("ident_masked", [P, P], BF16)
        ebias = sb("ebias", [P, 2], F32)
        csum = sb("csum", [P, 2, CH], F32)
        rsum = sb("rsum", [P, 2, 4], F32)
        z = sb("z", [P, 2, D], F32)
        stats = sb("stats", [P, nc.vector.BN_STATS_DIM], F32)
        moments = sb("moments", [P, nc.vector.BN_AGGR_DIM], F32)
        row_var = sb("row_var", [P, TILES], F32)
        var = sb("var", [P, TILES], F32)
        std = sb("std", [P, TILES], F32)
        rstd = sb("rstd", [P, TILES], F32)

        ps_s = ctx.enter_context(nc.psum_tensor("ps_s", [P, 2, W_SC], F32))
        ps_t = ctx.enter_context(nc.psum_tensor("ps_t", [P, 2, W_GR], F32))
        ps_o = ctx.enter_context(nc.psum_tensor("ps_o", [P, 2, W_GR], F32))

        in_landed = [sem(f"inp_landed{i}") for i in range(4)]
        x_landed = [sem(f"x_landed{i}") for i in range(4)]
        w_landed = sem("weights_landed")
        ident_ready = sem("ident_ready")
        vhi_ready = sem("value_high_ready")
        vlo_ready = sem("value_low_ready")
        kt_t = sem("keys_transposed")
        kt_hi = sem("keys_high_ready")
        kt_lo = sem("keys_low_ready")
        xt_t = sem("x_transposed")
        xt_sb = sem("x_transposed_copied")
        q_mm = sem("query_product_ready")
        q_hi = sem("query_high_ready")
        q_lo = sem("query_low_ready")
        adj_landed = [sem(f"adj_landed{i}") for i in range(PC)]
        mask_pool = sem("mask_ready_from_pool")
        mask_vec = sem("mask_ready_from_vector")
        pool_gate = sem("pool_gate")
        vec_gate = sem("vector_gate")
        act_gate = sem("scalar_gate")
        scores_ready = sem("scores_ready")
        masked_ready = sem("masked_ready")
        rowmax_ready = sem("rowmax_ready")
        ebias_ready = sem("exp_bias_ready")
        relu_ready = [sem("relu_ready_from_vector"), sem("relu_ready_from_scalar")]
        bit_ready = sem("no_edge_bit_ready")
        exp_ready = sem("exp_ready")
        transposed = sem("weights_transposed")
        hi_ready = sem("weight_high_ready")
        lo_ready = sem("weight_low_ready")
        pv_done = sem("value_product_done")
        xres_landed = [sem(f"residual_landed{i}") for i in range(2)]
        chain = sem("row_chain")
        var_ready = sem("variance_ready")
        std_ready = sem("std_ready")
        rstd_ready = sem("rstd_ready")
        rows_ready = sem("rows_normalised")
        x1t_t = sem("rows_transposed")
        x1t_sb = sem("rows_transposed_copied")
        w_prep = sem("weight_prep_product")
        w_copy = sem("weight_prep_copied")
        f1_ready = sem("f1_ready")
        wh_mm = sem("wh_product_ready")
        wh_hi = sem("wh_high_ready")
        wh_lo = sem("wh_low_ready")
        f2_mm = sem("f2_product_ready")
        f2_sb = sem("f2_copied")
        f2_split = sem("f2_split")
        stored = sem("stored")

        kt_hl = keys[:, :].bitcast(F16).rearrange("p (h n) -> p h n", h=2)
        q_hl = qx[:, :, :].bitcast(F16).rearrange("p t (h m) -> p t h m", h=2)
        in_nat = y[:, 0:N].rearrange("p (b d) -> p b d", d=D)
        x_nat = y[:, N:2 * N].rearrange("p (b d) -> p b d", d=D)
        x1t = y[:, 0:N]
        xt_tmp = [pt[:, i, :, :].rearrange("p h n -> p (h n)").bitcast(F32) for i in range(2)]
        x_dram = x.rearrange("(b p) d -> p b d", p=P)
        in_dram = inp.rearrange("(b p) d -> p b d", p=P)
        out_dram = out.rearrange("(b p) d -> p b d", p=P)
        adj_dram = adj.rearrange("(t p) (q n) -> t p q n", p=P, n=W_PC)
        QB = TILES // 4
        WHB = 3
        WHG = TILES // WHB

        def wait(eng, s, value):
            if not (isinstance(value, int) and value <= 0):
                eng.wait_ge(s, value)

        def y_chunk(c):
            return y[:, (c % RING) * W_SC:(c % RING + 1) * W_SC]

        block = ctx.enter_context(nc.Block())

        @block.sync
        def _(sp):
            sp.dma_start(w0_sb[:, :], w0).then_inc(w_landed, 16)
            for i in range(4):
                r = slice(i * QB, (i + 1) * QB)
                sp.dma_start(in_nat[:, r, :], in_dram[:, r, :]).then_inc(in_landed[i], 16)
                sp.dma_start(x_nat[:, r, :], x_dram[:, r, :]).then_inc(x_landed[i], 16)
            sp.dma_start(w1_sb[:, 0:D], w1).then_inc(w_landed, 16)
            for h in range(2):
                sp.dma_start(a_sb[:, h:h + 1], a[h * D:(h + 1) * D, :]).then_inc(w_landed, 16)

            def adjacency(layer, u):
                for j in range(2 * PC):
                    done = 2 * u + j // PC
                    if layer == 0 and j % PC == VEC_PIECE:
                        wait(sp, mask_vec, done)
                    elif layer == 0:
                        wait(sp, mask_pool, (PC - 1) * (done - 1) + j % PC + 1 if not isinstance(u, int) or done else 0)
                    elif isinstance(u, int) and done == 0:
                        sp.wait_ge(*((mask_vec, TILES) if j == VEC_PIECE else (mask_pool, POOL_L0)))
                    else:
                        sp.wait_ge(mask_pool, POOL_L0 + PC * (done - 1) + j % PC + 1)
                    sp.dma_start(adj_ring[:, j % PC, :], adj_dram[2 * u + j // PC, :, j % PC, :]
                                 ).then_inc(adj_landed[j % PC], 16)

            adjacency(0, 0)
            with sp.Fori(1, PAIRS) as u:
                adjacency(0, u)
            adjacency(1, 0)
            with sp.Fori(1, PAIRS) as u:
                adjacency(1, u)
            for i in range(4):
                r = slice(i * QB, (i + 1) * QB)
                sp.wait_ge(rows_ready, 4 + i + 1)
                sp.dma_start(out_dram[:, r, :], qx[:, r, :]).then_inc(stored, 16)
            sp.wait_ge(stored, 64)

        @block.gpsimd
        def _(pool):
            nc.gpsimd.memset(ident[:, :], 0.0).then_inc(ident_ready, 1)
            nc.gpsimd.memset(ones[:, :], 1.0).then_inc(ident_ready, 1)
            pool.wait_ge(ident_ready, 2)
            nc.gpsimd.affine_select(out=ident[:, :], in_=ident[:, :], compare_op=ALU.not_equal, fill=1.0, base=0,
                                    pattern=[[-1, P]], channel_multiplier=1).then_inc(ident_ready, 1)
            pool.wait_ge(ident_ready, 3)
            nc.gpsimd.tensor_scalar(ident_masked[:, :], ident[:, :], MASKED, 0.0, ALU.mult, ALU.add).then_inc(ident_ready, 1)
            nc.gpsimd.memset(part_sum[:, :], 0.0).then_inc(ident_ready, 1)
            pool.wait_ge(ident_ready, 5)
            for part in range(3):
                nc.gpsimd.memset(part_sum[32 * part:32 * part + 1, :], 1.0).then_inc(ident_ready, 1)
                pool.wait_ge(ident_ready, 6 + part)
            for i in range(4):
                r = slice(i * QB, (i + 1) * QB)
                pool.wait_ge(in_landed[i], 16)
                nc.gpsimd.tensor_scalar(val[:, r, 0:D], in_nat[:, r, :], SPLIT, None, ALU.mult).then_inc(vhi_ready, 1)

            def masks(u):
                for j in range(2 * PC):
                    if j % PC == VEC_PIECE:
                        continue
                    t, c = 2 * u + j // PC, j % PC
                    m = mask_ring[:, c, :]
                    pool.wait_ge(adj_landed[c], 16 * (t + 1))
                    wait(pool, masked_ready, CH * (t - 1) + CPP * (c + 1))
                    pool.sem_inc(pool_gate, 1)
                    nc.gpsimd.tensor_scalar(m, adj_ring[:, c, :], 0.0, None, ALU.is_le).then_inc(bit_ready, 1)
                    pool.wait_ge(bit_ready, (PC - 1) * t + c + 1)
                    pool.sem_inc(pool_gate, 1)
                    nc.gpsimd.tensor_scalar(m, m, MASKED, 0.0, ALU.mult, ALU.add).then_inc(mask_pool, 1)

            def bits(u):
                for j in range(2 * PC):
                    t, c = 2 * u + j // PC, j % PC
                    pool.wait_ge(adj_landed[c], 16 * (TILES + t + 1))
                    if isinstance(u, int) and t == 0:
                        pool.wait_ge(masked_ready, S_TOT - CH + CPP * (c + 1))
                    else:
                        pool.wait_ge(scores_ready, S_TOT + CH * (t - 1) + CPP * (c + 1))
                    pool.sem_inc(pool_gate, 1)
                    nc.gpsimd.tensor_scalar(mask_ring[:, c, :], adj_ring[:, c, :], 0.0, None, ALU.is_le
                                            ).then_inc(mask_pool, 1)

            masks(0)
            with pool.Fori(1, PAIRS) as u:
                masks(u)
            bits(0)
            with pool.Fori(1, PAIRS) as u:
                bits(u)

        @block.tensor
        def _(pe):
            def four_transposes(dst, src, g):
                for b in range(BLK):
                    last = nc.tensor.transpose(dst[:, b * P:(b + 1) * P], src[:, g * W_GR + b * P:g * W_GR + (b + 1) * P],
                                               ident[:, :])
                return last

            pe.wait_ge(ident_ready, 8)
            pe.wait_ge(w_landed, 64)
            for g in range(GR + 1):
                if g < GR:
                    pe.wait_ge(in_landed[g * BLK // QB], 16)
                    if g >= 2:
                        pe.wait_ge(kt_lo, g - 1)
                    four_transposes(ps_t[:, g % 2, :], y[:, 0:N], g).then_inc(kt_t, 1)
                    pe.wait_ge(x_landed[g * BLK // QB], 16)
                    if g >= 2:
                        pe.wait_ge(xt_sb, g - 1)
                    four_transposes(ps_s[:, 0, (g % 2) * W_GR:(g % 2 + 1) * W_GR], y[:, N:2 * N], g).then_inc(xt_t, 1)
                if g >= 1:
                    h = g - 1
                    pe.wait_ge(xt_sb, h + 1)
                    if h >= 2:
                        pe.wait_ge(q_lo, h - 1)
                    nc.tensor.matmul(ps_s[:, 1, (h % 2) * W_GR:(h % 2 + 1) * W_GR], w0_sb[:, :], xt_tmp[h % 2],
                                     start=True, stop=True).then_inc(q_mm, 1)
            pe.wait_ge(kt_lo, GR)
            nc.tensor.transpose(ps_t[:, 0, 0:P], w1_sb[:, 0:D], ident[:, :]).then_inc(w_prep, 1)
            pe.wait_ge(w_copy, 1)
            nc.tensor.matmul(ps_t[:, 1, 0:2], w1t[:, :], a_sb[:, :], start=True, stop=True).then_inc(w_prep, 1)
            pe.wait_ge(w_copy, 2)
            pe.wait_ge(q_lo, GR)

            def qk_half(n, i, h, tile):
                bank = ps_s[:, i % 2, h * W_GR:(h + 1) * W_GR]
                cols = slice((i % CH) * W_SC + h * W_GR, (i % CH) * W_SC + (h + 1) * W_GR)
                if h == 0:
                    wait(pe, masked_ready, n - 1)
                qh = q_hl[:, bass.ds(tile, 1), 0, :].rearrange("p o m -> p (o m)")
                ql = q_hl[:, bass.ds(tile, 1), 1, :].rearrange("p o m -> p (o m)")
                nc.tensor.matmul(bank, qh, kt_hl[:, 0, cols], start=True, stop=False)
                nc.tensor.matmul(bank, qh, kt_hl[:, 1, cols], start=False, stop=False)
                last = nc.tensor.matmul(bank, ql, kt_hl[:, 0, cols], start=False, stop=True)
                if h == 1:
                    last.then_inc(scores_ready, 1)

            def logit_half(n, i, h, tile):
                bank = ps_s[:, i % 2, h * W_GR:(h + 1) * W_GR]
                c = i % CH
                cols = slice(c * W_SC + h * W_GR, c * W_SC + (h + 1) * W_GR)
                piece, at = c // CPP, (c % CPP) * W_SC + h * W_GR
                if h == 0:
                    pe.wait_ge(masked_ready, n - 1)
                    pe.wait_ge(mask_pool, POOL_L0 + (tile - TILES) * PC + piece + 1)
                nc.tensor.matmul(bank, ident_masked[:, :], mask_ring[:, piece, at:at + W_GR], start=True, stop=False)
                last = nc.tensor.matmul(bank, part_sum[:, :], f2_parts[:, cols], start=False, stop=True)
                if h == 1:
                    last.then_inc(scores_ready, 1)

            def value_product(k, i):
                pe.wait_ge(lo_ready, k + 1)
                first, fin = i % GR == 0, i % GR == GR - 1
                o = ps_o[:, (i // GR) % 2, 0:2 * D]
                for b in range(BLK):
                    v = val[:, (i % GR) * BLK + b, :]
                    nc.tensor.matmul(o, pt[:, i % 4, 0, b * P:(b + 1) * P], v, start=first and b == 0, stop=False)
                    last = nc.tensor.matmul(o[:, 0:D], pt[:, i % 4, 1, b * P:(b + 1) * P], v[:, 0:D], start=False,
                                            stop=fin and b == BLK - 1)
                last.then_inc(pv_done, 1)

            def body(layer, u, first, last):
                s0, k0 = layer * S_TOT + RING * u, 2 * (layer * S_TOT + RING * u)
                for i in range(RING):
                    for h in range(2):
                        if not (last and i + QK_LEAD >= RING):
                            ahead = qk_half if layer == 0 else logit_half
                            ahead(s0 + i + QK_LEAD, i + QK_LEAD, h, layer * TILES + 2 * u + (i + QK_LEAD) // CH)
                        g = 2 * i + h
                        pe.wait_ge(exp_ready, s0 + i + 1)
                        wait(pe, lo_ready, k0 + g - 1)
                        four_transposes(ps_t[:, g % 2, :], y[:, :], g).then_inc(transposed, 1)
                        if not (first and g < PV_LAG):
                            j = (g - PV_LAG) % (2 * GR)
                            if j % GR == 0:
                                wait(pe, chain, CHAIN * (layer * TILES + 2 * u + (g - PV_LAG) // GR - 2) + OUT_TAKEN)
                            value_product(k0 + g - PV_LAG, j)

            for n in range(QK_LEAD):
                for h in range(2):
                    qk_half(n, n, h, n // CH)
            body(0, 0, True, False)
            with pe.Fori(1, PAIRS - 1) as u:
                body(0, u, False, False)
            body(0, PAIRS - 1, False, True)
            for j in range(2 * GR - PV_LAG, 2 * GR):
                value_product(2 * S_TOT - 2 * GR + j, j)

            for g in range(GR):
                pe.wait_ge(rows_ready, g * BLK // QB + 1)
                if g >= 2:
                    pe.wait_ge(x1t_sb, g - 1)
                four_transposes(ps_t[:, g % 2, :], qx[:, :, :].rearrange("p t d -> p (t d)"), g).then_inc(x1t_t, 1)
            for g in range(GR):
                pe.wait_ge(x1t_sb, g + 1)
                if g >= 2:
                    pe.wait_ge(f2_sb, g - 1)
                nc.tensor.matmul(ps_s[:, 0, (g % 2) * W_GR:(g % 2 + 1) * W_GR], wa2[:, :], x1t[:, g * W_GR:(g + 1) * W_GR],
                                 start=True, stop=True).then_inc(f2_mm, 1)
            for g in range(WHG):
                if g >= 2:
                    pe.wait_ge(wh_lo, g - 1)
                for b in range(WHB):
                    t = g * WHB + b
                    last = nc.tensor.matmul(ps_s[:, 1, (g % 2) * W_GR + b * (D + 1):(g % 2) * W_GR + (b + 1) * (D + 1)],
                                            x1t[:, t * P:(t + 1) * P], w1_sb[:, :], start=b == 0, stop=b == WHB - 1)
                last.then_inc(wh_mm, 1)
            pe.wait_ge(f2_split, 4)
            pe.wait_ge(wh_lo, WHG)
            for n in range(QK_LEAD):
                for h in range(2):
                    logit_half(S_TOT + n, n, h, TILES + n // CH)
            body(1, 0, True, False)
            with pe.Fori(1, PAIRS - 1) as u:
                body(1, u, False, False)
            body(1, PAIRS - 1, False, True)
            for j in range(2 * GR - PV_LAG, 2 * GR):
                value_product(4 * S_TOT - 2 * GR + j, j)

        @block.scalar
        def _(act):
            for g in range(GR):
                act.wait_ge(kt_t, g + 1)
                nc.scalar.activation(kt_hl[:, 0, g * W_GR:(g + 1) * W_GR], ps_t[:, g % 2, :], ACT.Copy, scale=SPLIT
                                     ).then_inc(kt_hi, 1)
                act.wait_ge(xt_t, g + 1)
                if g >= 2:
                    act.wait_ge(q_mm, g - 1)
                nc.scalar.activation(xt_tmp[g % 2], ps_s[:, 0, (g % 2) * W_GR:(g % 2 + 1) * W_GR], ACT.Copy
                                     ).then_inc(xt_sb, 1)
                act.wait_ge(q_mm, g + 1)
                nc.scalar.activation(q_hl[:, g * BLK:(g + 1) * BLK, 0, :],
                                     ps_s[:, 1, (g % 2) * W_GR:(g % 2 + 1) * W_GR].rearrange("p (t m) -> p t m", m=P),
                                     ACT.Copy, scale=Q_SPLIT / TEMPERATURE).then_inc(q_hi, 1)
            act.wait_ge(w_prep, 1)
            nc.scalar.activation(w1t[:, :], ps_t[:, 0, 0:P], ACT.Copy).then_inc(w_copy, 1)

            def high(k, i):
                act.wait_ge(transposed, k + 1)
                wait(act, pv_done, k - 3)
                nc.scalar.activation(pt[:, i % 4, 0, :], ps_t[:, i % 2, :], ACT.Copy).then_inc(hi_ready, 1)

            def exponential(layer, n, i, tile):
                slot = (i // CH) % 2
                if i % CH == 0:
                    act.wait_ge(rowmax_ready, tile + 1)
                    nc.scalar.activation(ebias[:, slot:slot + 1], rowmax[:, slot:slot + 1], ACT.Copy, bias=log(P_SCALE),
                                         scale=-1.0 / (SPLIT * Q_SPLIT) if layer == 0 else -1.0).then_inc(ebias_ready, 1)
                    act.wait_ge(ebias_ready, tile + 1)
                nc.scalar.activation(y_chunk(i), y_chunk(i), ACT.Exp, bias=ebias[:, slot:slot + 1],
                                     scale=1.0 / (SPLIT * Q_SPLIT) if layer == 0 else 1.0,
                                     accum_out=csum[:, slot, i % CH:i % CH + 1]).then_inc(exp_ready, 1)

            def rectify(n, i, tile):
                act.wait_ge(transposed, 2 * (n - RING + 1))
                act.sem_inc(act_gate, 1)
                nc.scalar.activation(y_chunk(i), keys[:, (i % CH) * W_SC:(i % CH + 1) * W_SC], ACT.Relu,
                                     bias=f1[:, bass.ds(tile, 1)]).then_inc(relu_ready[1], 1)

            def residual(tile, slot):
                wait(act, chain, CHAIN * (tile - 2) + OUT_TAKEN)
                act.dma_start(xres[:, slot, :], x_dram[:, bass.ds(tile, 1), :].rearrange("p o d -> p (o d)")
                              ).then_inc(xres_landed[slot], 16)

            def body(layer, u, last):
                s0 = layer * S_TOT + RING * u
                for i in range(RING):
                    high(2 * (s0 + i), 2 * i)
                    if layer == 0 and i % CH == 3:
                        residual(2 * u + i // CH, i // CH)
                    if not (last and i + EXP_LEAD >= RING):
                        exponential(layer, s0 + i + EXP_LEAD, i + EXP_LEAD, layer * TILES + 2 * u + (i + EXP_LEAD) // CH)
                    high(2 * (s0 + i) + 1, 2 * i + 1)
                    r = i + RELU_LEAD[1]
                    if layer == 1 and r % 2 == 1 and not (last and r >= RING):
                        rectify(s0 + r, r, 2 * u + r // CH)

            for n in range(EXP_LEAD):
                exponential(0, n, n, 0)
            body(0, 0, False)
            with act.Fori(1, PAIRS - 1) as u:
                body(0, u, False)
            body(0, PAIRS - 1, True)

            def deviation(layer):
                act.wait_ge(var_ready, layer + 1)
                nc.scalar.activation(std[:, :], var[:, :], ACT.Sqrt).then_inc(std_ready, 1)

            deviation(0)
            for g in range(GR):
                act.wait_ge(x1t_t, g + 1)
                nc.scalar.activation(x1t[:, g * W_GR:(g + 1) * W_GR], ps_t[:, g % 2, :], ACT.Copy).then_inc(x1t_sb, 1)
            for g in range(GR):
                act.wait_ge(f2_mm, g + 1)
                nc.scalar.activation(keys[:, g * W_GR:(g + 1) * W_GR], ps_s[:, 0, (g % 2) * W_GR:(g % 2 + 1) * W_GR],
                                     ACT.Copy, scale=1.0 - ALPHA).then_inc(f2_sb, 1)
            act.wait_ge(f2_sb, GR)
            nc.scalar.activation(f2_parts[:, :], keys[0:96, :], ACT.Copy, scale=ALPHA / (1.0 - ALPHA)).then_inc(f2_split, 1)
            for g in range(WHG):
                act.wait_ge(wh_mm, g + 1)
                wh = ps_s[:, 1, (g % 2) * W_GR:(g % 2) * W_GR + WHB * (D + 1)].rearrange("p (b d) -> p b d", b=WHB)
                nc.scalar.activation(f1[:, g * WHB:(g + 1) * WHB], wh[:, :, D], ACT.Copy, scale=1.0 - ALPHA).then_inc(f1_ready, 1)
                nc.scalar.activation(val[:, g * WHB:(g + 1) * WHB, 0:D], wh[:, :, 0:D], ACT.Copy, scale=SPLIT
                                     ).then_inc(wh_hi, 1)
            act.wait_ge(f1_ready, WHG)
            act.wait_ge(f2_split, 4)
            for n in range(1, RELU_LEAD[1], 2):
                rectify(S_TOT + n, n, n // CH)
            for n in range(EXP_LEAD):
                exponential(1, S_TOT + n, n, TILES)
            body(1, 0, False)
            with act.Fori(1, PAIRS - 1) as u:
                body(1, u, False)
            body(1, PAIRS - 1, True)
            deviation(1)

        @block.vector
        def _(dve):
            for g in range(GR):
                dve.wait_ge(kt_hi, g + 1)
                nc.vector.scalar_tensor_tensor(out=kt_hl[:, 1, g * W_GR:(g + 1) * W_GR], in0=ps_t[:, g % 2, :], scalar=SPLIT,
                                               in1=kt_hl[:, 0, g * W_GR:(g + 1) * W_GR], op0=ALU.mult,
                                               op1=ALU.subtract).then_inc(kt_lo, 1)
                dve.wait_ge(q_hi, g + 1)
                nc.vector.scalar_tensor_tensor(
                    out=q_hl[:, g * BLK:(g + 1) * BLK, 1, :],
                    in0=ps_s[:, 1, (g % 2) * W_GR:(g % 2 + 1) * W_GR].rearrange("p (t m) -> p t m", m=P),
                    scalar=Q_SPLIT / TEMPERATURE, in1=q_hl[:, g * BLK:(g + 1) * BLK, 0, :], op0=ALU.mult,
                    op1=ALU.subtract).then_inc(q_lo, 1)
            for i in range(4):
                r = slice(i * QB, (i + 1) * QB)
                dve.wait_ge(vhi_ready, i + 1)
                nc.vector.scalar_tensor_tensor(out=val[:, r, D:2 * D], in0=in_nat[:, r, :], scalar=SPLIT,
                                               in1=val[:, r, 0:D], op0=ALU.mult, op1=ALU.subtract
                                               ).then_inc(vlo_ready, 1)
            dve.wait_ge(vlo_ready, 4)
            dve.wait_ge(w_prep, 2)
            nc.vector.tensor_copy(w1_sb[:, D:D + 1], ps_t[:, 1, 0:1])
            nc.vector.tensor_copy(wa_sb[:, :], ps_t[:, 1, 0:2]).then_inc(w_copy, 1)
            dve.wait_ge(w_copy, 2)
            nc.vector.tensor_scalar(wa2[:, :], ones[:, :], wa_sb[:, 1:2], None, ALU.mult).then_inc(w_copy, 1)

            def mask_chunk(layer, n, i, tile):
                c, slot, piece = i % CH, (i // CH) % 2, (i % CH) // CPP
                m = mask_ring[:, piece, (c % CPP) * W_SC:(c % CPP + 1) * W_SC]
                dve.wait_ge(scores_ready, n + 1)
                if layer == 0:
                    if piece == VEC_PIECE:
                        dve.wait_ge(mask_vec, tile + 1)
                    elif c % CPP == 0:
                        dve.wait_ge(mask_pool, tile * (PC - 1) + piece + 1)
                    wait(dve, transposed, 2 * (n - RING + 1))
                    add = m
                else:
                    dve.wait_ge(relu_ready[i % 2], RING // 2 * (tile - TILES - i // CH) // 2 + i // 2 + 1)
                    add = y_chunk(i)
                dve.sem_inc(vec_gate, 1)
                nc.vector.tensor_tensor_reduce(out=y_chunk(i), in0=ps_s[:, i % 2, :], in1=add, scale=1.0, scalar=-3.0e38,
                                               op0=ALU.add, op1=ALU.max, accum_out=cmax[:, slot, c:c + 1]
                                               ).then_inc(masked_ready, 1)
                if c == CH - 1:
                    dve.wait_ge(masked_ready, n + 1)
                    nc.vector.reduce_max(rowmax[:, slot:slot + 1], cmax[:, slot, :], AX_X).then_inc(rowmax_ready, 1)

            def mask_piece(tile):
                dve.wait_ge(adj_landed[VEC_PIECE], 16 * (tile + 1))
                wait(dve, masked_ready, CH * tile)
                nc.vector.tensor_scalar(mask_ring[:, VEC_PIECE, :], adj_ring[:, VEC_PIECE, :], 0.0, MASKED, ALU.is_le,
                                        ALU.mult).then_inc(mask_vec, 1)

            def rectify(n, i, tile):
                dve.wait_ge(transposed, 2 * (n - RING + 1))
                nc.vector.tensor_scalar(y_chunk(i), keys[:, (i % CH) * W_SC:(i % CH + 1) * W_SC], f1[:, bass.ds(tile, 1)],
                                        0.0, ALU.add, ALU.max).then_inc(relu_ready[0], 1)

            def low(k, i):
                dve.wait_ge(hi_ready, k + 1)
                nc.vector.tensor_tensor(pt[:, i % 4, 1, :], ps_t[:, i % 2, :], pt[:, i % 4, 0, :], ALU.subtract
                                        ).then_inc(lo_ready, 1)

            def rows(layer, t, slot, part):
                at = layer * TILES + t
                dve.wait_ge(*((exp_ready, CH * (at + 1)) if part == 0 else (chain, CHAIN * at + part)))
                row = qx[:, bass.ds(t, 1), :].rearrange("p o d -> p (o d)")
                if part == 0:
                    nc.vector.reduce_sum(rsum[:, slot, 0:1], csum[:, slot, :], AX_X).then_inc(chain, 1)
                elif part == 1:
                    nc.vector.tensor_scalar(rsum[:, slot, 1:2], rsum[:, slot, 0:1], SPLIT, None, ALU.mult).then_inc(chain, 1)
                elif part == 2:
                    nc.vector.reciprocal(rsum[:, slot, 2:3], rsum[:, slot, 1:2]).then_inc(chain, 1)
                elif part == 3:
                    dve.wait_ge(pv_done, GR * (at + 1))
                    if layer == 0:
                        dve.wait_ge(xres_landed[slot], (t - slot) * 8 + 16)
                    res = xres[:, slot, :] if layer == 0 else row
                    nc.vector.scalar_tensor_tensor(out=z[:, 0, :], in0=ps_o[:, slot, 0:D], scalar=rsum[:, slot, 2:3],
                                                   in1=res, op0=ALU.mult, op1=ALU.add).then_inc(chain, 1)
                elif part == 4:
                    nc.vector.scalar_tensor_tensor(out=z[:, 1, :], in0=ps_o[:, slot, D:2 * D], scalar=rsum[:, slot, 2:3],
                                                   in1=z[:, 0, :], op0=ALU.mult, op1=ALU.add).then_inc(chain, 1)
                elif part == 5:
                    nc.vector.bn_stats(stats[:, :], z[:, 1, :]).then_inc(chain, 1)
                elif part == 6:
                    dve.sem_inc(vec_gate, 1)
                    nc.vector.bn_aggr(moments[:, :], stats[:, :]).then_inc(chain, 1)
                elif part == 7:
                    nc.vector.tensor_scalar(row, z[:, 1, :], moments[:, 0:1], None, ALU.subtract).then_inc(chain, 1)
                    nc.vector.tensor_copy(row_var[:, bass.ds(t, 1)], moments[:, 1:2]).then_inc(chain, 1)

            def body(layer, u, first, last):
                s0, t0 = layer * S_TOT + RING * u, layer * TILES + 2 * u
                for i in range(RING):
                    if not (last and i + MASK_LEAD >= RING):
                        if layer == 0 and (i + MASK_LEAD) % CH == 1:
                            mask_piece(2 * u + (i + MASK_LEAD) // CH)
                        mask_chunk(layer, s0 + i + MASK_LEAD, i + MASK_LEAD, t0 + (i + MASK_LEAD) // CH)
                    low(2 * (s0 + i), 2 * i)
                    r = i + RELU_LEAD[0]
                    if layer == 1 and r % 2 == 0 and not (last and r >= RING):
                        rectify(s0 + r, r, 2 * u + r // CH)
                    if not (first and i < CH) and 1 <= i % CH <= 4:
                        for part in (2 * (i % CH) - 2, 2 * (i % CH) - 1):
                            rows(layer, 2 * u + i // CH - 1, (i // CH + 1) % 2, part)
                            if part % 2 == 0:
                                low(2 * (s0 + i) + 1, 2 * i + 1)
                    else:
                        low(2 * (s0 + i) + 1, 2 * i + 1)

            def normalise(layer):
                dve.wait_ge(chain, CHAIN * TILES * (layer + 1))
                nc.vector.tensor_scalar(var[:, :], row_var[:, :], EPS, None, ALU.add).then_inc(var_ready, 1)
                dve.wait_ge(std_ready, layer + 1)
                nc.vector.reciprocal(rstd[:, :], std[:, :]).then_inc(rstd_ready, 1)
                dve.wait_ge(rstd_ready, layer + 1)
                for i in range(4):
                    r = slice(i * QB, (i + 1) * QB)
                    nc.vector.tensor_tensor(qx[:, r, :], qx[:, r, :], rstd[:, r].unsqueeze(2).to_broadcast([P, QB, D]),
                                            ALU.mult).then_inc(rows_ready, 1)

            for n in range(MASK_LEAD):
                if n % CH == 1:
                    mask_piece(n // CH)
                mask_chunk(0, n, n, n // CH)
            body(0, 0, True, False)
            with dve.Fori(1, PAIRS - 1) as u:
                body(0, u, False, False)
            body(0, PAIRS - 1, False, True)
            for part in range(CHAIN - 1):
                rows(0, TILES - 1, 1, part)
            normalise(0)
            for g in range(WHG):
                dve.wait_ge(wh_hi, g + 1)
                wh = ps_s[:, 1, (g % 2) * W_GR:(g % 2) * W_GR + WHB * (D + 1)].rearrange("p (b d) -> p b d", b=WHB)
                nc.vector.scalar_tensor_tensor(out=val[:, g * WHB:(g + 1) * WHB, D:2 * D], in0=wh[:, :, 0:D], scalar=SPLIT,
                                               in1=val[:, g * WHB:(g + 1) * WHB, 0:D], op0=ALU.mult,
                                               op1=ALU.subtract).then_inc(wh_lo, 1)
            dve.wait_ge(f2_split, 1)
            nc.vector.scalar_tensor_tensor(out=y[0:96, N:2 * N], in0=keys[0:96, :], scalar=ALPHA / (1.0 - ALPHA),
                                           in1=f2_parts[:, :], op0=ALU.mult, op1=ALU.subtract).then_inc(f2_split, 1)
            dve.wait_ge(f2_split, 2)
            for part in (1, 2):
                r = slice(32 * part, 32 * part + 32)
                last = nc.vector.tensor_copy(f2_parts[r, :], y[r, N:2 * N])
            last.then_inc(f2_split, 1)
            dve.wait_ge(f2_split, 3)
            nc.vector.tensor_tensor(f2_parts[64:96, :], y[64:96, N:2 * N], f2_parts[64:96, :], ALU.subtract
                                    ).then_inc(f2_split, 1)
            dve.wait_ge(f2_split, 4)
            dve.wait_ge(f1_ready, WHG)
            for n in range(0, RELU_LEAD[0], 2):
                rectify(S_TOT + n, n, n // CH)
            for n in range(MASK_LEAD):
                mask_chunk(1, S_TOT + n, n, TILES + n // CH)
            body(1, 0, True, False)
            with dve.Fori(1, PAIRS - 1) as u:
                body(1, u, False, False)
            body(1, PAIRS - 1, False, True)
            for part in range(CHAIN - 1):
                rows(1, TILES - 1, 1, part)
            normalise(1)


_INS = ['x', 'adj', 'L0_gnn_input', 'L0_gnn_weight', 'L1_gnn_W', 'L1_gnn_a']


def kernel(**inputs):
    import numpy as _np
    import concourse.bacc as _bacc
    from concourse import mybir as _mybir
    from concourse.bass_utils import run_bass_kernel_spmd as _run

    nc = _bacc.Bacc("TRN2", target_bir_lowering=False, num_devices=1)
    arrays, args = {}, []
    for name in _INS:
        arr = _np.ascontiguousarray(inputs[name])
        arrays[f"in_{name}_dram"] = arr
        args.append(nc.dram_tensor(f"in_{name}_dram", arr.shape, _mybir.dt.from_np(arr.dtype), kind="ExternalInput").ap())
    shape = inputs['x'].shape
    out = nc.dram_tensor("out_0_dram", shape, _mybir.dt.from_np(_np.dtype('float32')), kind="ExternalOutput").ap()
    two_layer_graph_attention(nc, *args, out)
    r = _run(nc, [arrays], core_ids=[0])
    return r.results[0]["out_0_dram"]
```

```python
from contextlib import ExitStack
from math import log

import concourse.bass as bass
from concourse import mybir

P = 128
W_SC = 1024
W_GR = 512
W_PC = 2048
SPLIT = 64.0
Q_SPLIT = 4.0
TEMPERATURE = 0.07
ALPHA = 0.2
EPS = 1e-5
P_SCALE = 4096.0
MASKED = -2.0 ** 100
QK_LEAD = 9
MASK_LEAD = 8
EXP_LEAD = 2
RELU_LEAD = (9, 10)
RELU_VEC = (1, 3, 5)
T_LEAD = 4
PV_LAG = 2

F32 = mybir.dt.float32
F16 = mybir.dt.float16
BF16 = mybir.dt.bfloat16
I32 = mybir.dt.int32
ALU = mybir.AluOpType
ACT = mybir.ActivationFunctionType
AX_X = mybir.AxisListType.X


def two_layer_graph_attention(nc, x, adj, inp, w0, w1, a, out):
    N, D = x.shape
    TILES = N // P
    CH = N // W_SC
    GR = N // W_GR
    PC = N // W_PC
    BLK = W_GR // P
    PAIRS = TILES // 2
    S_TOT = TILES * CH
    RING = 2 * CH
    CPP = W_PC // W_SC
    VEC_PIECE = PC - 1
    POOL_L0 = (TILES - 1) * (PC - 1)
    EARLY, EARLY_PARTS = TILES - 4, 4
    EARLY_STEP = 4
    X_PARTS = (0, 4, 24, TILES)
    CHAIN = 9
    OUT_TAKEN = 5
    assert D == P and TILES % 2 == 0

    with ExitStack() as ctx:
        def sb(name, shape, dt):
            return ctx.enter_context(nc.sbuf_tensor(name, shape, dt))

        def sem(name):
            return ctx.enter_context(nc.semaphore(name))

        adj_ring = sb("adj_ring", [P, PC, W_PC], I32)
        mask_ring = sb("mask_ring", [P, PC, W_PC], BF16)
        y = sb("y", [P, RING * W_SC], F32)
        keys = sb("keys", [P, N], F32)
        val = sb("val", [P, TILES, 2 * D], F16)
        qx = sb("qx", [P, TILES, D], F32)
        pt = sb("pt", [P, 4, 2, W_GR], F16)
        xres = sb("xres", [P, 2, D], F32)
        ident = sb("ident", [P, P], F32)
        w0_sb = sb("w0_sb", [P, D], F32)
        w1_sb = sb("w1_sb", [P, D + 1], F32)
        w1t = sb("w1t", [P, D], F32)
        a_sb = sb("a_sb", [P, 2], F32)
        wa2 = sb("wa2", [P, D], F32)
        ones = sb("ones", [P, D], F32)
        wa_sb = sb("wa_sb", [P, 2], F32)
        f1 = sb("f1", [P, TILES], F32)
        cmax = sb("cmax", [P, 2, CH], F32)
        rowmax = sb("rowmax", [P, 2], F32)
        f2_parts = sb("f2_parts", [64, N], F16)
        part_sum = sb("part_sum", [64, P], F16)
        ident_masked = sb("ident_masked", [P, P], BF16)
        ebias = sb("ebias", [P, 2], F32)
        csum = sb("csum", [P, 2, CH], F32)
        rsum = sb("rsum", [P, 2, 4], F32)
        z = sb("z", [P, 2, D], F32)
        stats = sb("stats", [P, nc.vector.BN_STATS_DIM], F32)
        moments = sb("moments", [P, nc.vector.BN_AGGR_DIM], F32)
        row_var = sb("row_var", [P, TILES], F32)
        var = sb("var", [P, TILES], F32)
        std = sb("std", [P, TILES], F32)
        rstd = sb("rstd", [P, TILES], F32)

        ps_s = ctx.enter_context(nc.psum_tensor("ps_s", [P, 2, W_SC], F32))
        ps_t = ctx.enter_context(nc.psum_tensor("ps_t", [P, 2, W_GR], F32))
        ps_o = ctx.enter_context(nc.psum_tensor("ps_o", [P, 2, W_GR], F32))

        in_landed = [sem(f"inp_landed{i}") for i in range(4)]
        x_landed = [sem(f"x_landed{i}") for i in range(3)]
        w0_landed = sem("w0_landed")
        w1_landed = sem("w1_and_a_landed")
        ident_ready = sem("ident_ready")
        vhi_ready = sem("value_high_ready")
        vlo_ready = sem("value_low_ready")
        kt_t = sem("keys_transposed")
        kt_hi = sem("keys_high_ready")
        kt_lo = sem("keys_low_ready")
        xt_t = sem("x_transposed")
        xt_sb = sem("x_transposed_copied")
        q_mm = sem("query_product_ready")
        q_hi = sem("query_high_ready")
        q_lo = sem("query_low_ready")
        adj_landed = [sem(f"adj_landed{i}") for i in range(PC)]
        mask_pool = sem("mask_ready_from_pool")
        mask_vec = sem("mask_ready_from_vector")
        pool_gate = sem("pool_gate")
        vec_gate = sem("vector_gate")
        act_gate = sem("scalar_gate")
        scores_ready = sem("scores_ready")
        masked_ready = sem("masked_ready")
        rowmax_ready = sem("rowmax_ready")
        ebias_ready = sem("exp_bias_ready")
        relu_ready = [sem("relu_ready_from_vector"), sem("relu_ready_from_scalar")]
        bit_ready = sem("no_edge_bit_ready")
        exp_ready = sem("exp_ready")
        transposed = sem("weights_transposed")
        hi_ready = sem("weight_high_ready")
        lo_ready = sem("weight_low_ready")
        pv_done = sem("value_product_done")
        xres_landed = [sem(f"residual_landed{i}") for i in range(2)]
        chain = sem("row_chain")
        var_ready = sem("variance_ready")
        std_ready = sem("std_ready")
        rstd_ready = sem("rstd_ready")
        early_ready = sem("early_rows_normalised")
        last_ready = sem("last_rows_normalised")
        x1t_t = sem("rows_transposed")
        x1t_sb = sem("rows_transposed_copied")
        w_prep = sem("weight_prep_product")
        w_copy = sem("weight_prep_copied")
        f1_ready = sem("f1_ready")
        wh_mm = sem("wh_product_ready")
        wh_hi = sem("wh_high_ready")
        wh_lo = sem("wh_low_ready")
        f2_mm = sem("f2_product_ready")
        f2_sb = sem("f2_copied")
        f2_hi = sem("f2_high_ready")
        f2_lo = sem("f2_low_ready")
        stored = sem("stored")

        kt_hl = keys[:, :].bitcast(F16).rearrange("p (h n) -> p h n", h=2)
        q_hl = qx[:, :, :].bitcast(F16).rearrange("p t (h m) -> p t h m", h=2)
        in_nat = y[:, N:2 * N].rearrange("p (b d) -> p b d", d=D)
        x1t = y[:, N:2 * N]
        xt_tmp = [pt[:, i, :, :].rearrange("p h n -> p (h n)").bitcast(F32) for i in range(2)]
        x_dram = x.rearrange("(b p) d -> p b d", p=P)
        in_dram = inp.rearrange("(b p) d -> p b d", p=P)
        out_dram = out.rearrange("(b p) d -> p b d", p=P)
        adj_dram = adj.rearrange("(t p) (q n) -> t p q n", p=P, n=W_PC)
        QB = TILES // 4
        CB = W_SC // P
        WHB = 3
        WHG = TILES // WHB
        RELU_ACT = [c for c in range(CH) if c not in RELU_VEC]
        EP = EARLY // EARLY_PARTS
        row_parts = [slice(i * EP, (i + 1) * EP) for i in range(EARLY_PARTS)] + [slice(EARLY, TILES)]

        def wait(eng, s, value):
            if not (isinstance(value, int) and value <= 0):
                eng.wait_ge(s, value)

        def y_chunk(c):
            return y[:, (c % RING) * W_SC:(c % RING + 1) * W_SC]

        block = ctx.enter_context(nc.Block())

        @block.sync
        def _(sp):
            def adjacency_piece(layer, u, j):
                done = 2 * u + j // PC
                if layer == 0 and isinstance(done, int) and done == 0:
                    pass
                elif layer == 0 and j % PC == VEC_PIECE:
                    sp.wait_ge(mask_vec, PC + done - 1)
                elif layer == 0 and isinstance(done, int) and done == 1:
                    sp.wait_ge(mask_vec, j % PC + 1)
                elif layer == 0:
                    sp.wait_ge(mask_pool, (PC - 1) * (done - 2) + j % PC + 1)
                elif isinstance(u, int) and done == 0:
                    sp.wait_ge(*((mask_vec, PC + TILES - 1) if j == VEC_PIECE else (mask_pool, POOL_L0)))
                else:
                    sp.wait_ge(mask_pool, POOL_L0 + PC * (done - 1) + j % PC + 1)
                sp.dma_start(adj_ring[:, j % PC, :], adj_dram[2 * u + j // PC, :, j % PC, :]
                             ).then_inc(adj_landed[j % PC], 16)

            def adjacency(layer, u, first=0):
                for j in range(first, 2 * PC):
                    adjacency_piece(layer, u, j)

            def quarter(i):
                r = slice(i * QB, (i + 1) * QB)
                sp.dma_start(in_nat[:, r, :], in_dram[:, r, :]).then_inc(in_landed[i], 16)

            def x_part(i):
                r = slice(X_PARTS[i], X_PARTS[i + 1])
                sp.dma_start(qx[:, r, :], x_dram[:, r, :]).then_inc(x_landed[i], 16)

            sp.dma_start(w1_sb[:, 0:D], w1).then_inc(w1_landed, 16)
            for h in range(2):
                sp.dma_start(a_sb[:, h:h + 1], a[h * D:(h + 1) * D, :]).then_inc(w1_landed, 16)
            sp.dma_start(w0_sb[:, :], w0).then_inc(w0_landed, 16)
            x_part(0)
            quarter(0)
            adjacency_piece(0, 0, 0)
            quarter(1)
            adjacency_piece(0, 0, 1)
            quarter(2)
            quarter(3)
            adjacency_piece(0, 0, 2)
            x_part(1)
            adjacency_piece(0, 0, PC)
            x_part(2)
            adjacency(0, 0, PC + 1)
            with sp.Fori(1, PAIRS) as u:
                adjacency(0, u)
            adjacency(1, 0)
            with sp.Fori(1, PAIRS) as u:
                adjacency(1, u)
            for i, r in enumerate(row_parts):
                sp.wait_ge(*((early_ready, EARLY_PARTS + i + 1) if i < EARLY_PARTS else (last_ready, 2)))
                sp.dma_start(out_dram[:, r, :], qx[:, r, :]).then_inc(stored, 16)
            sp.wait_ge(stored, 16 * len(row_parts))

        @block.gpsimd
        def _(pool):
            nc.gpsimd.memset(ident[:, :], 0.0).then_inc(ident_ready, 1)
            nc.gpsimd.memset(ones[:, :], 1.0).then_inc(ident_ready, 1)
            pool.wait_ge(ident_ready, 2)
            nc.gpsimd.affine_select(out=ident[:, :], in_=ident[:, :], compare_op=ALU.not_equal, fill=1.0, base=0,
                                    pattern=[[-1, P]], channel_multiplier=1).then_inc(ident_ready, 1)
            pool.wait_ge(ident_ready, 3)
            nc.gpsimd.tensor_scalar(ident_masked[:, :], ident[:, :], MASKED, 0.0, ALU.mult, ALU.add).then_inc(ident_ready, 1)
            nc.gpsimd.memset(part_sum[:, :], 0.0).then_inc(ident_ready, 1)
            pool.wait_ge(ident_ready, 5)
            for part in range(2):
                nc.gpsimd.memset(part_sum[32 * part:32 * part + 1, :], 1.0).then_inc(ident_ready, 1)
                pool.wait_ge(ident_ready, 6 + part)

            def masks(u):
                for j in range(2 * PC):
                    if j % PC == VEC_PIECE or (isinstance(u, int) and j < PC):
                        continue
                    t, c = 2 * u + j // PC, j % PC
                    m = mask_ring[:, c, :]
                    pool.wait_ge(adj_landed[c], 16 * (t + 1))
                    wait(pool, masked_ready, CH * (t - 1) + CPP * (c + 1))
                    pool.sem_inc(pool_gate, 1)
                    nc.gpsimd.tensor_scalar(m, adj_ring[:, c, :], 0.0, None, ALU.is_le).then_inc(bit_ready, 1)
                    pool.wait_ge(bit_ready, (PC - 1) * (t - 1) + c + 1)
                    pool.sem_inc(pool_gate, 1)
                    nc.gpsimd.tensor_scalar(m, m, MASKED, 0.0, ALU.mult, ALU.add).then_inc(mask_pool, 1)

            def bits(u):
                for j in range(2 * PC):
                    t, c = 2 * u + j // PC, j % PC
                    pool.wait_ge(adj_landed[c], 16 * (TILES + t + 1))
                    if isinstance(u, int) and t == 0:
                        pool.wait_ge(masked_ready, S_TOT - CH + CPP * (c + 1))
                    else:
                        pool.wait_ge(scores_ready, S_TOT + CH * (t - 1) + CPP * (c + 1))
                    pool.sem_inc(pool_gate, 1)
                    nc.gpsimd.tensor_scalar(mask_ring[:, c, :], adj_ring[:, c, :], 0.0, None, ALU.is_le
                                            ).then_inc(mask_pool, 1)

            def early_rows(layer):
                pool.wait_ge(rstd_ready, 2 * layer + 1)
                for r in row_parts[:EARLY_PARTS]:
                    nc.gpsimd.tensor_tensor(qx[:, r, :], qx[:, r, :],
                                            rstd[:, r].unsqueeze(2).to_broadcast([P, r.stop - r.start, D]),
                                            ALU.mult).then_inc(early_ready, 1)

            masks(0)
            with pool.Fori(1, PAIRS) as u:
                masks(u)
            early_rows(0)
            bits(0)
            with pool.Fori(1, PAIRS) as u:
                bits(u)
            early_rows(1)

        @block.tensor
        def _(pe):
            def four_transposes(dst, src, g):
                for b in range(BLK):
                    last = nc.tensor.transpose(dst[:, b * P:(b + 1) * P], src[:, g * W_GR + b * P:g * W_GR + (b + 1) * P],
                                               ident[:, :])
                return last

            def qk_half(n, i, h, tile):
                bank = ps_s[:, i % 2, h * W_GR:(h + 1) * W_GR]
                cols = slice((i % CH) * W_SC + h * W_GR, (i % CH) * W_SC + (h + 1) * W_GR)
                if h == 0:
                    wait(pe, masked_ready, n - 1)
                qh = q_hl[:, bass.ds(tile, 1), 0, :].rearrange("p o m -> p (o m)")
                ql = q_hl[:, bass.ds(tile, 1), 1, :].rearrange("p o m -> p (o m)")
                nc.tensor.matmul(bank, qh, kt_hl[:, 0, cols], start=True, stop=False)
                nc.tensor.matmul(bank, qh, kt_hl[:, 1, cols], start=False, stop=False)
                last = nc.tensor.matmul(bank, ql, kt_hl[:, 0, cols], start=False, stop=True)
                if h == 1:
                    last.then_inc(scores_ready, 1)

            def logit_half(n, i, h, tile):
                bank = ps_s[:, i % 2, h * W_GR:(h + 1) * W_GR]
                c = i % CH
                cols = slice(c * W_SC + h * W_GR, c * W_SC + (h + 1) * W_GR)
                piece, at = c // CPP, (c % CPP) * W_SC + h * W_GR
                if h == 0:
                    pe.wait_ge(masked_ready, n - 1)
                    pe.wait_ge(mask_pool, POOL_L0 + (tile - TILES) * PC + piece + 1)
                nc.tensor.matmul(bank, ident_masked[:, :], mask_ring[:, piece, at:at + W_GR], start=True, stop=False)
                last = nc.tensor.matmul(bank, part_sum[:, :], f2_parts[:, cols], start=False, stop=True)
                if h == 1:
                    last.then_inc(scores_ready, 1)

            def value_product(k, i):
                pe.wait_ge(lo_ready, k + 1)
                first, fin = i % GR == 0, i % GR == GR - 1
                o = ps_o[:, (i // GR) % 2, 0:2 * D]
                for b in range(BLK):
                    v = val[:, (i % GR) * BLK + b, :]
                    nc.tensor.matmul(o, pt[:, i % 4, 0, b * P:(b + 1) * P], v, start=first and b == 0, stop=False)
                    last = nc.tensor.matmul(o[:, 0:D], pt[:, i % 4, 1, b * P:(b + 1) * P], v[:, 0:D], start=False,
                                            stop=fin and b == BLK - 1)
                last.then_inc(pv_done, 1)

            def body(layer, u, first, last):
                s0, k0 = layer * S_TOT + RING * u, 2 * (layer * S_TOT + RING * u)
                for i in range(RING):
                    for h in range(2):
                        if not (last and i + QK_LEAD >= RING):
                            ahead = qk_half if layer == 0 else logit_half
                            ahead(s0 + i + QK_LEAD, i + QK_LEAD, h, layer * TILES + 2 * u + (i + QK_LEAD) // CH)
                        g = 2 * i + h
                        pe.wait_ge(exp_ready, s0 + i + 1)
                        wait(pe, lo_ready, k0 + g - 1)
                        four_transposes(ps_t[:, g % 2, :], y[:, :], g).then_inc(transposed, 1)
                        if not (first and g < PV_LAG):
                            j = (g - PV_LAG) % (2 * GR)
                            if j % GR == 0:
                                wait(pe, chain, CHAIN * (layer * TILES + 2 * u + (g - PV_LAG) // GR - 2) + OUT_TAKEN)
                            value_product(k0 + g - PV_LAG, j)

            pe.wait_ge(ident_ready, 3)
            pe.wait_ge(w1_landed, 48)
            nc.tensor.transpose(ps_s[:, 0, 0:P], w1_sb[:, 0:D], ident[:, :]).then_inc(w_prep, 1)
            pe.wait_ge(w_copy, 1)
            nc.tensor.matmul(ps_s[:, 0, W_GR:W_GR + 2], w1t[:, :], a_sb[:, :], start=True, stop=True).then_inc(w_prep, 1)
            x_flat = qx[:, :, :].rearrange("p t d -> p (t d)")

            def x_transposes(g):
                pe.wait_ge(x_landed[sum(g * BLK >= b for b in X_PARTS[1:])], 16)
                wait(pe, xt_sb, g)
                four_transposes(ps_o[:, 0, :], x_flat, g).then_inc(xt_t, 1)

            def query_product(g):
                pe.wait_ge(xt_sb, g + 1)
                if g >= 3:
                    pe.wait_ge(q_lo, g - 1)
                bank = ps_o[:, 1, :] if g == 0 else ps_t[:, g % 2, :]
                nc.tensor.matmul(bank, w0_sb[:, :], xt_tmp[g % 2], start=True, stop=True).then_inc(q_mm, 1)

            pe.wait_ge(w0_landed, 16)
            x_transposes(0)
            query_product(0)
            for g in range(GR + 2):
                if g < GR:
                    pe.wait_ge(in_landed[g * BLK // QB], 16)
                    if g >= 2:
                        pe.wait_ge(kt_lo, g - 1)
                    four_transposes(ps_t[:, g % 2, :], y[:, N:2 * N], g).then_inc(kt_t, 1)
                if g >= 2:
                    if g == 2:
                        pe.wait_ge(w_copy, 2)
                        pe.wait_ge(q_lo, 1)
                    pe.wait_ge(kt_lo, g - 1)
                    qk_half((g - 2) // 2, (g - 2) // 2, g % 2, 0)
            ahead = [(n, h) for n in range(CH, QK_LEAD) for h in range(2)]
            x_transposes(1)
            for g in range(1, GR):
                if g < GR - 1:
                    x_transposes(g + 1)
                query_product(g)
                if g >= 4 and ahead:
                    n, h = ahead.pop(0)
                    qk_half(n, n, h, 1)
            pe.wait_ge(q_lo, GR)
            body(0, 0, True, False)
            with pe.Fori(1, PAIRS - 1) as u:
                body(0, u, False, False)
            body(0, PAIRS - 1, False, True)
            for j in range(2 * GR - PV_LAG, 2 * GR):
                value_product(2 * S_TOT - 2 * GR + j, j)

            def row_transposes(g):
                if (g + 1) * BLK > EARLY:
                    pe.wait_ge(last_ready, 1)
                else:
                    pe.wait_ge(early_ready, -(-(g + 1) * BLK // EP))
                if g >= 2:
                    pe.wait_ge(x1t_sb, g - 1)
                four_transposes(ps_t[:, g % 2, :], x_flat, g).then_inc(x1t_t, 1)

            def wh_product(g):
                if g >= 2:
                    pe.wait_ge(wh_lo, g - 1)
                for b in range(WHB):
                    t = g * WHB + b
                    last = nc.tensor.matmul(ps_o[:, g % 2, b * (D + 1):(b + 1) * (D + 1)], x1t[:, t * P:(t + 1) * P],
                                            w1_sb[:, :], start=b == 0, stop=b == WHB - 1)
                last.then_inc(wh_mm, 1)

            for g in range(T_LEAD):
                row_transposes(g)
            for g in range(GR):
                if g + T_LEAD < GR:
                    row_transposes(g + T_LEAD)
                pe.wait_ge(x1t_sb, g + 1)
                if g >= 2:
                    pe.wait_ge(f2_sb, g - 1)
                nc.tensor.matmul(ps_o[:, g % 2, :], wa2[:, :], x1t[:, g * W_GR:(g + 1) * W_GR],
                                 start=True, stop=True).then_inc(f2_mm, 1)
            pe.wait_ge(ident_ready, 7)
            pe.wait_ge(f2_sb, GR)
            for g in range(WHG):
                wh_product(g)
                n, h = g // 2, g % 2
                if n < CH + 2:
                    if h == 0 and n < CH:
                        pe.wait_ge(f2_lo, -(-(n + 1) * W_SC // (N // 4)))
                    logit_half(S_TOT + n, n, h, TILES + n // CH)
            for n in range(CH + 2, QK_LEAD):
                for h in range(2):
                    logit_half(S_TOT + n, n, h, TILES + n // CH)
            pe.wait_ge(wh_lo, WHG)
            body(1, 0, True, False)
            with pe.Fori(1, PAIRS - 1) as u:
                body(1, u, False, False)
            body(1, PAIRS - 1, False, True)
            for j in range(2 * GR - PV_LAG, 2 * GR):
                value_product(4 * S_TOT - 2 * GR + j, j)

        @block.scalar
        def _(act):
            act.wait_ge(w_prep, 1)
            nc.scalar.activation(w1t[:, :], ps_s[:, 0, 0:P], ACT.Copy).then_inc(w_copy, 1)

            def x_copy(g):
                act.wait_ge(xt_t, g + 1)
                wait(act, q_mm, g - 1)
                nc.scalar.activation(xt_tmp[g % 2], ps_o[:, 0, :], ACT.Copy).then_inc(xt_sb, 1)

            def query_high(g):
                act.wait_ge(q_mm, g + 1)
                bank = ps_o[:, 1, :] if g == 0 else ps_t[:, g % 2, :]
                nc.scalar.activation(q_hl[:, g * BLK:(g + 1) * BLK, 0, :], bank.rearrange("p (t m) -> p t m", m=P),
                                     ACT.Copy, scale=Q_SPLIT / TEMPERATURE).then_inc(q_hi, 1)

            x_copy(0)
            query_high(0)
            for g in range(GR):
                act.wait_ge(kt_t, g + 1)
                nc.scalar.activation(kt_hl[:, 0, g * W_GR:(g + 1) * W_GR], ps_t[:, g % 2, :], ACT.Copy, scale=SPLIT
                                     ).then_inc(kt_hi, 1)
                if g % 2 == 1:
                    c = slice(g // 2 * CB, (g // 2 + 1) * CB)
                    nc.scalar.activation(val[:, c, 0:D], in_nat[:, c, :], ACT.Copy, scale=SPLIT).then_inc(vhi_ready, 1)
            x_copy(1)

            def high(k, i):
                act.wait_ge(transposed, k + 1)
                wait(act, pv_done, k - 3)
                nc.scalar.activation(pt[:, i % 4, 0, :], ps_t[:, i % 2, :], ACT.Copy).then_inc(hi_ready, 1)

            def exponential(layer, n, i, tile):
                slot = (i // CH) % 2
                if i % CH == 0:
                    act.wait_ge(rowmax_ready, tile + 1)
                    nc.scalar.activation(ebias[:, slot:slot + 1], rowmax[:, slot:slot + 1], ACT.Copy, bias=log(P_SCALE),
                                         scale=-1.0 / (SPLIT * Q_SPLIT) if layer == 0 else -1.0).then_inc(ebias_ready, 1)
                    act.wait_ge(ebias_ready, tile + 1)
                nc.scalar.activation(y_chunk(i), y_chunk(i), ACT.Exp, bias=ebias[:, slot:slot + 1],
                                     scale=1.0 / (SPLIT * Q_SPLIT) if layer == 0 else 1.0,
                                     accum_out=csum[:, slot, i % CH:i % CH + 1]).then_inc(exp_ready, 1)

            def rectify(n, i, tile):
                act.wait_ge(transposed, 2 * (n - RING + 1))
                act.sem_inc(act_gate, 1)
                nc.scalar.activation(y_chunk(i), keys[:, (i % CH) * W_SC:(i % CH + 1) * W_SC], ACT.Relu,
                                     bias=f1[:, bass.ds(tile, 1)]).then_inc(relu_ready[1], 1)

            def residual(tile, slot):
                wait(act, chain, CHAIN * (tile - 2) + OUT_TAKEN)
                act.dma_start(xres[:, slot, :], x_dram[:, bass.ds(tile, 1), :].rearrange("p o d -> p (o d)")
                              ).then_inc(xres_landed[slot], 16)

            def deviation(part):
                act.wait_ge(var_ready, part + 1)
                r = slice(0, EARLY) if part % 2 == 0 else slice(EARLY, TILES)
                nc.scalar.activation(std[:, r], var[:, r], ACT.Sqrt).then_inc(std_ready, 1)

            def body(layer, u, last):
                s0 = layer * S_TOT + RING * u
                for i in range(RING):
                    high(2 * (s0 + i), 2 * i)
                    if layer == 0 and i % CH == 3:
                        residual(2 * u + i // CH, i // CH)
                    if not (last and i + EXP_LEAD >= RING):
                        exponential(layer, s0 + i + EXP_LEAD, i + EXP_LEAD, layer * TILES + 2 * u + (i + EXP_LEAD) // CH)
                    high(2 * (s0 + i) + 1, 2 * i + 1)
                    if last and i == EARLY_STEP:
                        deviation(2 * layer)
                    r = i + RELU_LEAD[1]
                    if layer == 1 and r % CH in RELU_ACT and not (last and r >= RING):
                        rectify(s0 + r, r, 2 * u + r // CH)

            for g in range(1, GR):
                if g < GR - 1:
                    x_copy(g + 1)
                query_high(g)
                if g in (6, 8):
                    n = (g - 6) // 2
                    exponential(0, n, n, 0)
            body(0, 0, False)
            with act.Fori(1, PAIRS - 1) as u:
                body(0, u, False)
            body(0, PAIRS - 1, True)

            def f2_high(q):
                act.wait_ge(f2_sb, (q + 1) * GR // 4)
                c = slice(q * (N // 4), (q + 1) * (N // 4))
                nc.scalar.activation(f2_parts[:, c], keys[0:64, c], ACT.Copy, scale=ALPHA / (1.0 - ALPHA)
                                     ).then_inc(f2_hi, 1)

            for g in range(GR):
                act.wait_ge(x1t_t, g + 1)
                nc.scalar.activation(x1t[:, g * W_GR:(g + 1) * W_GR], ps_t[:, g % 2, :], ACT.Copy).then_inc(x1t_sb, 1)
                if g == 1:
                    deviation(1)
                if g in (8, 10):
                    f2_high((g - 8) // 2)
            f2_high(2)
            f2_high(3)
            for g in range(WHG):
                act.wait_ge(wh_mm, g + 1)
                wh = ps_o[:, g % 2, 0:WHB * (D + 1)].rearrange("p (b d) -> p b d", b=WHB)
                nc.scalar.activation(f1[:, g * WHB:(g + 1) * WHB], wh[:, :, D], ACT.Copy, scale=1.0 - ALPHA
                                     ).then_inc(f1_ready, 1)
                nc.scalar.activation(val[:, g * WHB:(g + 1) * WHB, 0:D], wh[:, :, 0:D], ACT.Copy, scale=SPLIT
                                     ).then_inc(wh_hi, 1)
                if g % 2 == 0 and g // 2 < len(RELU_ACT):
                    n = RELU_ACT[g // 2]
                    act.wait_ge(f1_ready, 1)
                    rectify(S_TOT + n, n, 0)
            act.wait_ge(f1_ready, WHG)
            exponential(1, S_TOT, 0, TILES)
            own = [n for n in range(CH, RELU_LEAD[1]) if n % CH in RELU_ACT]
            for n in own[:1]:
                rectify(S_TOT + n, n, 1)
            exponential(1, S_TOT + 1, 1, TILES)
            for n in own[1:]:
                rectify(S_TOT + n, n, 1)
            body(1, 0, False)
            with act.Fori(1, PAIRS - 1) as u:
                body(1, u, False)
            body(1, PAIRS - 1, True)
            deviation(3)

        @block.vector
        def _(dve):
            dve.wait_ge(w_prep, 2)
            nc.vector.tensor_copy(w1_sb[:, D:D + 1], ps_s[:, 0, W_GR:W_GR + 1])
            nc.vector.tensor_copy(wa_sb[:, :], ps_s[:, 0, W_GR:W_GR + 2]).then_inc(w_copy, 1)
            dve.wait_ge(w_copy, 2)
            dve.wait_ge(ident_ready, 2)
            nc.vector.tensor_scalar(wa2[:, :], ones[:, :], wa_sb[:, 1:2], None, ALU.mult).then_inc(w_copy, 1)

            def query_low(g):
                dve.wait_ge(q_hi, g + 1)
                bank = ps_o[:, 1, :] if g == 0 else ps_t[:, g % 2, :]
                nc.vector.scalar_tensor_tensor(
                    out=q_hl[:, g * BLK:(g + 1) * BLK, 1, :], in0=bank.rearrange("p (t m) -> p t m", m=P),
                    scalar=Q_SPLIT / TEMPERATURE, in1=q_hl[:, g * BLK:(g + 1) * BLK, 0, :], op0=ALU.mult,
                    op1=ALU.subtract).then_inc(q_lo, 1)

            def key_low(g):
                dve.wait_ge(kt_hi, g + 1)
                nc.vector.scalar_tensor_tensor(out=kt_hl[:, 1, g * W_GR:(g + 1) * W_GR], in0=ps_t[:, g % 2, :], scalar=SPLIT,
                                               in1=kt_hl[:, 0, g * W_GR:(g + 1) * W_GR], op0=ALU.mult,
                                               op1=ALU.subtract).then_inc(kt_lo, 1)

            def value_low(c):
                dve.wait_ge(vhi_ready, c + 1)
                b = slice(c * CB, (c + 1) * CB)
                nc.vector.scalar_tensor_tensor(out=val[:, b, D:2 * D], in0=in_nat[:, b, :], scalar=SPLIT,
                                               in1=val[:, b, 0:D], op0=ALU.mult, op1=ALU.subtract
                                               ).then_inc(vlo_ready, 1)

            def mask_chunk(layer, n, i, tile):
                c, slot, piece = i % CH, (i // CH) % 2, (i % CH) // CPP
                dve.wait_ge(scores_ready, n + 1)
                if layer == 0:
                    if isinstance(tile, int) and tile == 0:
                        dve.wait_ge(mask_vec, piece + 1)
                    elif piece == VEC_PIECE:
                        dve.wait_ge(mask_vec, PC + tile)
                    elif c % CPP == 0:
                        dve.wait_ge(mask_pool, (tile - 1) * (PC - 1) + piece + 1)
                    wait(dve, transposed, 2 * (n - RING + 1))
                    add = mask_ring[:, piece, (c % CPP) * W_SC:(c % CPP + 1) * W_SC]
                else:
                    own, maker = (RELU_VEC, 0) if c in RELU_VEC else (RELU_ACT, 1)
                    dve.wait_ge(relu_ready[maker], len(own) * (tile - TILES) + own.index(c) + 1)
                    add = y_chunk(i)
                dve.sem_inc(vec_gate, 1)
                nc.vector.tensor_tensor_reduce(out=y_chunk(i), in0=ps_s[:, i % 2, :], in1=add, scale=1.0, scalar=-3.0e38,
                                               op0=ALU.add, op1=ALU.max, accum_out=cmax[:, slot, c:c + 1]
                                               ).then_inc(masked_ready, 1)
                if c == CH - 1:
                    dve.wait_ge(masked_ready, n + 1)
                    nc.vector.reduce_max(rowmax[:, slot:slot + 1], cmax[:, slot, :], AX_X).then_inc(rowmax_ready, 1)

            def mask_piece(tile, piece=VEC_PIECE):
                dve.wait_ge(adj_landed[piece], 16 * (tile + 1))
                wait(dve, masked_ready, CH * tile)
                nc.vector.tensor_scalar(mask_ring[:, piece, :], adj_ring[:, piece, :], 0.0, MASKED, ALU.is_le,
                                        ALU.mult).then_inc(mask_vec, 1)

            def rectify(n, i, tile):
                dve.wait_ge(transposed, 2 * (n - RING + 1))
                nc.vector.tensor_scalar(y_chunk(i), keys[:, (i % CH) * W_SC:(i % CH + 1) * W_SC], f1[:, bass.ds(tile, 1)],
                                        0.0, ALU.add, ALU.max).then_inc(relu_ready[0], 1)

            def low(k, i):
                dve.wait_ge(hi_ready, k + 1)
                nc.vector.tensor_tensor(pt[:, i % 4, 1, :], ps_t[:, i % 2, :], pt[:, i % 4, 0, :], ALU.subtract
                                        ).then_inc(lo_ready, 1)

            def rows(layer, t, slot, part):
                at = layer * TILES + t
                dve.wait_ge(*((exp_ready, CH * (at + 1)) if part == 0 else (chain, CHAIN * at + part)))
                row = qx[:, bass.ds(t, 1), :].rearrange("p o d -> p (o d)")
                if part == 0:
                    nc.vector.reduce_sum(rsum[:, slot, 0:1], csum[:, slot, :], AX_X).then_inc(chain, 1)
                elif part == 1:
                    nc.vector.tensor_scalar(rsum[:, slot, 1:2], rsum[:, slot, 0:1], SPLIT, None, ALU.mult).then_inc(chain, 1)
                elif part == 2:
                    nc.vector.reciprocal(rsum[:, slot, 2:3], rsum[:, slot, 1:2]).then_inc(chain, 1)
                elif part == 3:
                    dve.wait_ge(pv_done, GR * (at + 1))
                    if layer == 0:
                        dve.wait_ge(xres_landed[slot], (t - slot) * 8 + 16)
                    res = xres[:, slot, :] if layer == 0 else row
                    nc.vector.scalar_tensor_tensor(out=z[:, 0, :], in0=ps_o[:, slot, 0:D], scalar=rsum[:, slot, 2:3],
                                                   in1=res, op0=ALU.mult, op1=ALU.add).then_inc(chain, 1)
                elif part == 4:
                    nc.vector.scalar_tensor_tensor(out=z[:, 1, :], in0=ps_o[:, slot, D:2 * D], scalar=rsum[:, slot, 2:3],
                                                   in1=z[:, 0, :], op0=ALU.mult, op1=ALU.add).then_inc(chain, 1)
                elif part == 5:
                    nc.vector.bn_stats(stats[:, :], z[:, 1, :]).then_inc(chain, 1)
                elif part == 6:
                    dve.sem_inc(vec_gate, 1)
                    nc.vector.bn_aggr(moments[:, :], stats[:, :]).then_inc(chain, 1)
                elif part == 7:
                    nc.vector.tensor_scalar(row, z[:, 1, :], moments[:, 0:1], None, ALU.subtract).then_inc(chain, 1)
                    nc.vector.tensor_copy(row_var[:, bass.ds(t, 1)], moments[:, 1:2]).then_inc(chain, 1)

            def body(layer, u, first, last):
                s0, t0 = layer * S_TOT + RING * u, layer * TILES + 2 * u
                for i in range(RING):
                    if not (last and i + MASK_LEAD >= RING):
                        if layer == 0 and (i + MASK_LEAD) % CH == 1:
                            mask_piece(2 * u + (i + MASK_LEAD) // CH)
                        mask_chunk(layer, s0 + i + MASK_LEAD, i + MASK_LEAD, t0 + (i + MASK_LEAD) // CH)
                    low(2 * (s0 + i), 2 * i)
                    r = i + RELU_LEAD[0]
                    if layer == 1 and r % CH in RELU_VEC and not (last and r >= RING):
                        rectify(s0 + r, r, 2 * u + r // CH)
                    if not (first and i < CH) and 1 <= i % CH <= 4:
                        for part in (2 * (i % CH) - 2, 2 * (i % CH) - 1):
                            rows(layer, 2 * u + i // CH - 1, (i // CH + 1) % 2, part)
                            if part % 2 == 0:
                                low(2 * (s0 + i) + 1, 2 * i + 1)
                    else:
                        low(2 * (s0 + i) + 1, 2 * i + 1)
                    if last and i == EARLY_STEP:
                        variance(2 * layer)
                    elif last and i == EARLY_STEP + 1:
                        inverse_deviation(2 * layer)

            def variance(part):
                r = slice(0, EARLY) if part % 2 == 0 else slice(EARLY, TILES)
                dve.wait_ge(chain, CHAIN * (part // 2 * TILES + r.stop))
                wait(dve, std_ready, part)
                nc.vector.tensor_scalar(var[:, r], row_var[:, r], EPS, None, ALU.add).then_inc(var_ready, 1)

            def inverse_deviation(part):
                r = slice(0, EARLY) if part % 2 == 0 else slice(EARLY, TILES)
                dve.wait_ge(std_ready, part + 1)
                nc.vector.reciprocal(rstd[:, r], std[:, r]).then_inc(rstd_ready, 1)

            def last_rows(layer):
                for part in range(CHAIN - 1):
                    rows(layer, TILES - 1, 1, part)
                variance(2 * layer + 1)
                inverse_deviation(2 * layer + 1)
                dve.wait_ge(rstd_ready, 2 * layer + 2)
                r = row_parts[-1]
                nc.vector.tensor_tensor(qx[:, r, :], qx[:, r, :],
                                        rstd[:, r].unsqueeze(2).to_broadcast([P, r.stop - r.start, D]),
                                        ALU.mult).then_inc(last_ready, 1)

            query_low(0)
            for g in range(GR):
                key_low(g)
                if g % 4 == 2:
                    mask_piece(0, g // 4)
                if g % 2 == 1 and g >= 3:
                    mask_chunk(0, (g - 3) // 2, (g - 3) // 2, 0)
            mask_chunk(0, CH - 1, CH - 1, 0)
            for g in range(1, GR):
                query_low(g)
                if g <= CH:
                    value_low(g - 1)
                if g == 7:
                    dve.wait_ge(vlo_ready, CH)
                if g in (7, 9):
                    mask_chunk(0, CH + (g - 7) // 2, CH + (g - 7) // 2, 1)
                elif g == 8:
                    mask_piece(1)
            body(0, 0, True, False)
            with dve.Fori(1, PAIRS - 1) as u:
                body(0, u, False, False)
            body(0, PAIRS - 1, False, True)
            last_rows(0)
            def f2_low(q):
                dve.wait_ge(f2_hi, q + 1)
                c = slice(q * (N // 4), (q + 1) * (N // 4))
                nc.vector.scalar_tensor_tensor(out=f2_parts[32:64, c], in0=keys[32:64, c], scalar=ALPHA / (1.0 - ALPHA),
                                               in1=f2_parts[32:64, c], op0=ALU.mult, op1=ALU.subtract).then_inc(f2_lo, 1)

            for g in range(GR):
                dve.wait_ge(f2_mm, g + 1)
                nc.vector.tensor_scalar(keys[:, g * W_GR:(g + 1) * W_GR], ps_o[:, g % 2, :], 1.0 - ALPHA, None, ALU.mult
                                        ).then_inc(f2_sb, 1)
                if g >= 5 and (g - 5) % (GR // 4) == 0:
                    f2_low((g - 5) // (GR // 4))
            f2_low(3)
            for g in range(WHG):
                dve.wait_ge(wh_hi, g + 1)
                wh = ps_o[:, g % 2, 0:WHB * (D + 1)].rearrange("p (b d) -> p b d", b=WHB)
                v = val[:, g * WHB:(g + 1) * WHB, :]
                nc.vector.scalar_tensor_tensor(out=v[:, :, D:2 * D], in0=wh[:, :, 0:D], scalar=SPLIT, in1=v[:, :, 0:D],
                                               op0=ALU.mult, op1=ALU.subtract).then_inc(wh_lo, 1)
                if g % 2 == 0 and g // 2 < len(RELU_VEC):
                    dve.wait_ge(f1_ready, 1)
                    rectify(S_TOT + RELU_VEC[g // 2], RELU_VEC[g // 2], 0)
                if g % 2 == 1 and g < GR:
                    mask_chunk(1, S_TOT + g // 2, g // 2, TILES)
            for n in range(CH, RELU_LEAD[0]):
                if n % CH in RELU_VEC:
                    rectify(S_TOT + n, n, n // CH)
                if n < MASK_LEAD:
                    mask_chunk(1, S_TOT + n, n, TILES + n // CH)
            body(1, 0, True, False)
            with dve.Fori(1, PAIRS - 1) as u:
                body(1, u, False, False)
            body(1, PAIRS - 1, False, True)
            last_rows(1)


_INS = ['x', 'adj', 'L0_gnn_input', 'L0_gnn_weight', 'L1_gnn_W', 'L1_gnn_a']


def kernel(**inputs):
    import numpy as _np
    import concourse.bacc as _bacc
    from concourse import mybir as _mybir
    from concourse.bass_utils import run_bass_kernel_spmd as _run

    nc = _bacc.Bacc("TRN2", target_bir_lowering=False, num_devices=1)
    arrays, args = {}, []
    for name in _INS:
        arr = _np.ascontiguousarray(inputs[name])
        arrays[f"in_{name}_dram"] = arr
        args.append(nc.dram_tensor(f"in_{name}_dram", arr.shape, _mybir.dt.from_np(arr.dtype), kind="ExternalInput").ap())
    shape = inputs['x'].shape
    out = nc.dram_tensor("out_0_dram", shape, _mybir.dt.from_np(_np.dtype('float32')), kind="ExternalOutput").ap()
    two_layer_graph_attention(nc, *args, out)
    r = _run(nc, [arrays], core_ids=[0])
    return r.results[0]["out_0_dram"]
```
